# Optimizing a Trainium2 kernel written in Bass

```python
import numpy as np
import jax
import jax.numpy as jnp

def _softmax(x, axis=-1):
    return jax.nn.softmax(x, axis=axis)

def _gelu(x):
    return jax.nn.gelu(x, approximate=True)

def _silu(x):
    return jax.nn.silu(x)

def _sigmoid(x):
    return jax.nn.sigmoid(x)

def _layernorm(x, axis=-1, eps=1e-05):
    m = jnp.mean(x, axis=axis, keepdims=True)
    v = jnp.var(x, axis=axis, keepdims=True)
    return (x - m) / jnp.sqrt(v + eps)

def _scatter_add(tgt, idx, src, axis=0):
    return tgt.at[idx].add(src)

def _segment_sum(src, seg, n):
    return jax.ops.segment_sum(src, seg, n)
kernel_name = 'mk_lm_tower_d1_tok_ids2048_r4_72dcc9'

def setup_inputs(seed: int=0):
    np.random.seed(seed)
    _w = jnp.asarray

    def _rec_inputs():
        import jax
        import jax.numpy as jnp
        _rk = jax.random.key(seed)
        x = jax.random.randint(jax.random.fold_in(_rk, 1), (32, 256), 0, 32000, jnp.int32)
        return x
    x = _rec_inputs()

    def _L0_tok_setup():
        import jax, jax.numpy as jnp
        import numpy as np
        VOCAB = 32000
        DIM = 512
        B, S = (8, 1024)
        TOKEN_IDS = np.arange(31996, 32000)
        key = jax.random.key(seed)
        k1, k2, k3 = jax.random.split(key, 3)
        weight = jax.random.normal(k1, (VOCAB, DIM), dtype=jnp.float32) * 0.02
        extra = jax.random.normal(k2, (len(TOKEN_IDS), DIM), dtype=jnp.float32) * 0.02
        input_ids = jax.random.randint(k3, (B, S), 0, VOCAB, dtype=jnp.int32)
        input_ids = input_ids.at[:, :len(TOKEN_IDS)].set(jnp.asarray(TOKEN_IDS, dtype=jnp.int32)[None, :])
        return {'input_ids': input_ids, 'weight': weight, 'extra': extra}
    _L0_tok_all = _L0_tok_setup()
    _L0_tok_in = {k: v for k, v in _L0_tok_all.items() if k in ('weight', 'extra')}
    del _L0_tok_all

    def _L0_attn_setup():
        import jax, jax.numpy as jnp
        import numpy as np
        B, T, C = (4, 1024, 512)
        key = jax.random.key(seed)
        k0, k1, k2, k3 = jax.random.split(key, 4)
        s = 0.02
        x = jax.random.normal(k0, (B, T, C), jnp.float32)
        W_act = jax.random.normal(k1, (C, 2 * C), jnp.float32) * s
        W_val = jax.random.normal(k2, (C, C), jnp.float32) * s
        W_rec = jax.random.normal(k3, (C, 2 * C), jnp.float32) * s
        return {'x': x, 'W_act': W_act, 'W_val': W_val, 'W_rec': W_rec}
    _L0_attn_all = _L0_attn_setup()
    _L0_attn_in = {k: v for k, v in _L0_attn_all.items() if k in ('W_act', 'W_val', 'W_rec')}
    del _L0_attn_all

    def _L0_ffn_setup():
        import jax, jax.numpy as jnp
        import numpy as np

        def ternary_quantize(t, threshold, scale):
            return jnp.where(t > threshold, scale, jnp.where(t < -threshold, -scale, 0.0)).astype(t.dtype)
        key = jax.random.key(seed)
        k1, k2, k3 = jax.random.split(key, 3)
        B, S, D = (4, 1024, 512)
        x = jax.random.normal(k1, (B, S, D), dtype=jnp.float32)
        weight = jax.random.normal(k2, (D, D), dtype=jnp.float32) * 0.02
        rram_variation = jax.random.normal(k3, (D, D), dtype=jnp.float32) * 0.05
        return {'x': x, 'weight': weight, 'rram_variation': rram_variation}
    _L0_ffn_all = _L0_ffn_setup()
    _L0_ffn_in = {k: v for k, v in _L0_ffn_all.items() if k in ('weight', 'rram_variation')}
    del _L0_ffn_all
    return {'x': x, 'L0_tok_weight': _L0_tok_in['weight'], 'L0_tok_extra': _L0_tok_in['extra'], 'L0_attn_W_act': _L0_attn_in['W_act'], 'L0_attn_W_val': _L0_attn_in['W_val'], 'L0_attn_W_rec': _L0_attn_in['W_rec'], 'L0_ffn_weight': _L0_ffn_in['weight'], 'L0_ffn_rram_variation': _L0_ffn_in['rram_variation']}

def reference(x, L0_tok_weight, L0_tok_extra, L0_attn_W_act, L0_attn_W_val, L0_attn_W_rec, L0_ffn_weight, L0_ffn_rram_variation):
    import jax
    import jax.numpy as jnp

    def _L0_tok_ref(input_ids, weight, extra):
        import jax, jax.numpy as jnp
        import numpy as np
        VOCAB = 32000
        DIM = 512
        B, S = (8, 1024)
        TOKEN_IDS = np.arange(31996, 32000)
        n_over = extra.shape[0]
        over_idx = jnp.full((VOCAB,), -1, dtype=jnp.int32).at[jnp.asarray(TOKEN_IDS, dtype=jnp.int32)].set(jnp.arange(n_over, dtype=jnp.int32))
        oi = over_idx[input_ids]
        base = weight[input_ids]
        repl = extra[jnp.clip(oi, 0, n_over - 1)]
        return jnp.where((oi >= 0)[..., None], repl, base)

    def _L0_attn_ref(x, W_act, W_val, W_rec):
        import jax, jax.numpy as jnp
        import numpy as np
        B, T, C = (4, 1024, 512)
        Bx, Tx, Cx = x.shape
        shifted = jnp.concatenate([jnp.zeros_like(x[:, :1]), x[:, :-1]], axis=1)
        ct = jnp.concatenate([shifted, x], axis=-1)
        xv = jax.nn.sigmoid(jax.nn.relu(jnp.einsum('btk,ck->btc', ct, W_act)))
        z = xv.reshape(Bx, Tx, Cx // 2, 2)
        re, im = (z[..., 0], z[..., 1])
        mag = jnp.sqrt(re * re + im * im)
        m = jax.lax.cummax(mag, axis=1)
        re, im = (re / m, im / m)

        def cmul(a, b):
            ar, ai = a
            br, bi = b
            return (ar * br - ai * bi, ar * bi + ai * br)
        re_p, im_p = jax.lax.associative_scan(cmul, (re, im), axis=1)
        kv = jnp.stack([re_p, im_p], axis=-1).reshape(Bx, Tx, Cx)
        r = jax.nn.sigmoid(jax.nn.relu(jnp.einsum('btk,ck->btc', ct, W_rec)))
        return jnp.einsum('btk,ck->btc', kv, W_val) * r ** 4

    def _L0_ffn_ref(x, weight, rram_variation):
        import jax, jax.numpy as jnp
        import numpy as np

        def ternary_quantize(t, threshold, scale):
            return jnp.where(t > threshold, scale, jnp.where(t < -threshold, -scale, 0.0)).astype(t.dtype)
        TH_X, SC_X = (0.33, 0.5)
        TH_W, SC_W = (0.2, 0.6)
        x_q = ternary_quantize(x, TH_X, SC_X)
        w_q = ternary_quantize(weight, TH_W, SC_W)
        w_rram = w_q + rram_variation
        return jnp.einsum('bsd,od->bso', x_q, w_rram)
    h = _L0_tok_ref(x, L0_tok_weight, L0_tok_extra)
    h = h + _L0_attn_ref(_layernorm(h, axis=-1), L0_attn_W_act, L0_attn_W_val, L0_attn_W_rec)
    h = h + _L0_ffn_ref(_layernorm(h, axis=-1), L0_ffn_weight, L0_ffn_rram_variation)
    return h

_drawn_inputs = setup_inputs


def setup_inputs(seed=0):
    import zlib

    import numpy as np

    out = dict(_drawn_inputs(seed))
    spreads = {}
    factors = {'L0_tok_extra': 93.112}
    for name, (base, spread) in spreads.items():
        noise = np.random.default_rng([zlib.crc32(name.encode()), seed]).standard_normal(out[name].shape)
        drawn = base * np.exp(spread * noise) if base else spread * noise
        out[name] = jnp.asarray(drawn.astype(out[name].dtype))
    for name, factor in factors.items():
        out[name] = (out[name] * factor).astype(out[name].dtype)
    return out
```

```python
from contextlib import ExitStack

import numpy as np

import concourse.bass as bass
from concourse import mybir

ALU = mybir.AluOpType
ACT = mybir.ActivationFunctionType
AX = mybir.AxisListType
F32 = mybir.dt.float32
F16 = mybir.dt.float16
I32 = mybir.dt.int32

P = 128
BATCH, SEQ, DIM, VOCAB, EXTRA = 32, 256, 512, 32000, 4
TOKENS = BATCH * SEQ
BLOCK = 512
NBLK = TOKENS // BLOCK
NSEQ = BLOCK // SEQ
TT = BLOCK // P
KT = DIM // P
PAIRS = KT // 2
SEQ_COLS = SEQ + 2

EPS = 1e-5
X_SCALE = 256.0
KV_SCALE = 2.0 ** 14
W_EXP = 13
EXP_MASK = 0x7F800000
MAGIC = 1.5 * 2.0 ** 23
TWO_PI = float(np.float32(2 * np.pi))
HALF_PI = float(np.float32(np.pi / 2))
PI_IN = 3.1415925
X_THRESHOLD, W_THRESHOLD, W_LEVEL = 0.33, 0.2, 0.6

SD, SA = 14, 9


def is_block(i, n):
    return isinstance(i, int) and i == n


def phase_steps():
    steps, total = np.zeros(SEQ, np.float32), 0.0
    for t in range(SEQ):
        want = ((t + 1) % 8) * np.pi / 4
        if want > np.pi:
            want -= 2 * np.pi
        steps[t] = np.float32(want - total)
        total += float(steps[t])
    return steps


def tower_kernel(nc, x, table, w_act, w_val, w_rec, w_ffn, w_var, steps, out):
    with ExitStack() as ctx:
        def sb(name, shape, dt=F32):
            return ctx.enter_context(nc.sbuf_tensor(name, shape, dt))

        def sem(name):
            return ctx.enter_context(nc.semaphore(name))

        bank = [ctx.enter_context(nc.psum_tensor(f"bank{b}", [P, 512], F32)) for b in range(8)]

        ident = sb("ident", [P, P])
        ident16 = sb("ident16", [P, P], F16)
        step_row = sb("step_row", [P, SEQ])
        half = sb("half", [P, TT])
        half_pi = sb("half_pi", [P, 1])
        wact_t = [sb(f"wact_{n}", [P, 2 * KT, DIM], F16) for n in ("hi", "lo")]
        wrec_t = [sb(f"wrec_{n}", [P, 2 * KT, DIM], F16) for n in ("hi", "lo")]
        wval_t = [sb(f"wval_{n}", [P, KT, DIM], F16) for n in ("hi", "lo")]
        wffn_t = [sb(f"wffn_{n}", [P, KT, DIM], F16) for n in ("hi", "lo")]
        ids_i = sb("ids_i", [TOKENS // P, P], I32)
        ids_f = sb("ids_f", [TOKENS // P, P])
        over = sb("over", [P, TOKENS // P])
        rows = sb("rows", [P, TOKENS // P], I32)
        rows_now = sb("rows_now", [P, 2, TT], I32)
        h = sb("h", [P, 2, TT, DIM])
        h1 = sb("h1", [P, 2, TT, DIM])
        xn = sb("xn", [P, TT, DIM])
        xT = [[sb(f"xT_{n}{b}", [P, KT, NSEQ, SEQ_COLS], F16) for n in ("hi", "lo")] for b in range(2)]
        z = sb("z", [P, PAIRS, 2, BLOCK])
        ab = sb("ab", [P, PAIRS, 2, BLOCK])
        cd = sb("cd", [P, PAIRS, 2, BLOCK])
        kv = [sb(f"kv_{n}", [P, PAIRS, 2, BLOCK], F16) for n in ("hi", "lo")]
        r4 = sb("r4", [P, TT, DIM])
        y = sb("y", [P, TT, DIM])
        below = sb("below", [P, TT, DIM], F16)
        q = sb("q", [P, TT, DIM], F16)
        qT = sb("qT", [P, KT, BLOCK], F16)
        stats = [sb(f"stats{n}", [P, TT, 6]) for n in (1, 2)]
        mv = [sb(f"mv{n}", [P, TT, 2]) for n in (1, 2)]
        ve = [sb(f"ve{n}", [P, TT]) for n in (1, 2)]
        rstd = [sb(f"rstd{n}", [P, TT]) for n in (1, 2)]
        nbias = [sb(f"nbias{n}", [P, TT]) for n in (1, 2)]
        w_stage = sb("w_stage", [P, 4096])
        wact_n = w_stage[:, :].rearrange("p (c k) -> p c k", c=KT)
        wrec_n = h1[:, :, :, :].rearrange("p a t n -> p (a t n)").rearrange("p (c k) -> p c k", c=KT)
        wval_n = w_stage[:, 0:2048].rearrange("p (c k) -> p c k", c=KT)
        wffn_n = w_stage[:, 2048:4096]
        wvar_n = y[:, :, :].rearrange("p c k -> p (c k)")
        level = sb("level", [P, 2048])
        NW = 4
        amax = sb("amax", [P, NW])
        amax_all = sb("amax_all", [P, NW])
        amax_pos = sb("amax_pos", [P, NW])
        pow2 = sb("pow2", [P, NW])
        wscale = sb("wscale", [P, NW])
        unscale = sb("unscale", [P, NW])
        UNSCALE = [2.0 ** -W_EXP / X_SCALE, 2.0 ** -W_EXP / X_SCALE,
                   2.0 ** -W_EXP / KV_SCALE, 2.0 ** -W_EXP * 0.5]

        s_wdma = [sem(f"s_wdma{n}") for n in ("act", "rec", "val", "ffn", "var")]
        s_ids, s_steps = sem("s_ids_loaded"), sem("s_steps_loaded")
        s_const = sem("s_constants")
        s_idsf, s_idsT, s_over, s_rows = sem("s_ids_float"), sem("s_ids_T"), sem("s_over"), sem("s_rows")
        s_idf, s_id16 = sem("s_ident"), sem("s_ident16")
        s_pad = sem("s_xT_zero_cols")
        s_amax, s_amaxall = sem("s_amax"), sem("s_amax_all")
        s_sc = sem("s_scale_steps")
        s_lvl = sem("s_ffn_levels")
        s_wps, s_whi, s_wlo = sem("s_w_transposed"), sem("s_w_hi"), sem("s_w_lo")
        s_now, s_gath = sem("s_rows_now"), sem("s_gathered")
        s_bn = [sem(f"s_bn{n}") for n in (1, 2)]
        s_held = [sem(f"s_wait_carrier_{e}") for e in ("pool", "dve")]
        s_mv = [sem(f"s_mv{n}") for n in (1, 2)]
        s_ve = [sem(f"s_ve{n}") for n in (1, 2)]
        s_rstd = [sem(f"s_rstd{n}") for n in (1, 2)]
        s_nb = [sem(f"s_nbias{n}") for n in (1, 2)]
        s_xn = sem("s_xn")
        s_xps, s_xhi, s_xlo = sem("s_x_transposed"), sem("s_xT_hi"), sem("s_xT_lo")
        s_aps, s_z = sem("s_act_product"), sem("s_z")
        s_sd = [sem(f"s_scan_dve{p}") for p in range(PAIRS)]
        s_sa = [sem(f"s_scan_act{p}") for p in range(PAIRS)]
        s_kvhi, s_kvlo = sem("s_kv_hi"), sem("s_kv_lo")
        s_vps, s_t, s_h1 = sem("s_val_product"), sem("s_val_gated"), sem("s_h1")
        s_y, s_below, s_q = sem("s_y"), sem("s_below"), sem("s_q")
        s_qps, s_qT = sem("s_q_transposed"), sem("s_qT")
        s_rps, s_rsig, s_rmax = sem("s_rec_product"), sem("s_r_sigmoid"), sem("s_r_max")
        s_r2, s_r4 = sem("s_r2"), sem("s_r4")
        s_fps, s_fin = sem("s_ffn_product"), sem("s_final")
        s_out = [sem(f"s_stored{b}") for b in range(2)]

        out_v = out.rearrange("b s d -> (b s) d")
        ACT_W, REC_W, VAL_W, FFN_W = range(NW)
        W_FIRST = {ACT_W: 0, REC_W: 2 * KT, VAL_W: 4 * KT, FFN_W: 5 * KT}
        W_BANKS = {ACT_W: 2 * KT, REC_W: 2 * KT, VAL_W: KT, FFN_W: KT}
        W_DST = {ACT_W: wact_t, REC_W: wrec_t, VAL_W: wval_t, FFN_W: wffn_t}
        W_ALL = 6 * KT

        def w_bank(n):
            return bank[n] if n < 2 * KT else bank[n % 4]

        block = ctx.enter_context(nc.Block())

        def iterations(engine, body):
            body(0, 0, False, True)
            body(1, 1, True, True)
            body(2, 0, True, True)
            with engine.Fori(3, NBLK - 2, 2) as i:
                body(i, 1, True, True)
                body(i + 1, 0, True, True)
            body(NBLK - 1, 1, True, True)
            body(NBLK, 0, True, False)

        @block.sync
        def _(sp):
            sp.dma_start(ids_i[:, :], x.rearrange("b (a p) -> (b a) p", p=P)).then_inc(s_ids, 16)
            sp.dma_start(wact_n.rearrange("p (r two) k -> p r two k", two=2),
                         w_act.rearrange("(r p two) k -> p r two k", p=P, two=2)).then_inc(s_wdma[0], 16)
            sp.dma_start(step_row[:, :], steps[:, :]).then_inc(s_steps, 16)
            sp.dma_start(wrec_n, w_rec.rearrange("(c p) k -> p c k", p=P)).then_inc(s_wdma[1], 16)
            sp.dma_start(wvar_n.rearrange("p (c k) -> p c k", c=KT),
                         w_var.rearrange("(c p) k -> p c k", p=P)).then_inc(s_wdma[4], 16)
            sp.wait_ge(s_wps, 2 * KT)
            sp.wait_ge(s_amax, 1)
            sp.dma_start(wval_n, w_val.rearrange("(c p) k -> p c k", p=P)).then_inc(s_wdma[2], 16)
            sp.dma_start(wffn_n.rearrange("p (c k) -> p c k", c=KT),
                         w_ffn.rearrange("(c p) k -> p c k", p=P)).then_inc(s_wdma[3], 16)

            def store(i, par, second, first):
                if not second:
                    return
                sp.wait_ge(s_fin, 4 * i)
                sp.dma_start(out_v[bass.ds((i - 1) * BLOCK, BLOCK), :].rearrange("(t p) d -> p t d", p=P),
                             h1[:, 1 - par, :, :]).then_inc(s_out[1 - par], 16)

            iterations(sp, store)
            for b in range(2):
                sp.wait_ge(s_out[b], 8 * NBLK)

        @block.gpsimd
        def _(pool):
            pool.memset(ident[:, :], 0.0).then_inc(s_idf, 1)
            pool.memset(half[:, :], -0.5).then_inc(s_const, 1)
            pool.wait_ge(s_idf, 1)
            pool.affine_select(out=ident[:, :], in_=ident[:, :], compare_op=ALU.not_equal, fill=1.0,
                               base=0, pattern=[[-1, P]], channel_multiplier=1).then_inc(s_idf, 1)
            pool.wait_ge(s_idf, 2)
            pool.tensor_copy(ident16[:, :], ident[:, :]).then_inc(s_id16, 1)

            def gather(i, par):
                if is_block(i, 0):
                    pool.wait_ge(s_rows, 1)
                pool.tensor_copy(rows_now[:, par, :], rows[:, bass.ds(i * TT, TT)]).then_inc(s_now, 1)
                pool.wait_ge(s_now, i + 1)
                pool.sem_inc(s_held[0], 1)
                for t in range(TT):
                    pool.indirect_dma_start(
                        h[:, par, t, :], None, table,
                        bass.IndirectOffsetOnAxis(ap=rows_now[:, par, t:t + 1], axis=0),
                    ).then_inc(s_gath, 16)

            def inverse_sqrt(n, i):
                pool.wait_ge(s_ve[n], i + 1)
                pool.tensor_tensor(rstd[n][:, :], ve[n][:, :], half[:, :], ALU.pow).then_inc(s_rstd[n], 1)

            def weight_max(w):
                pool.wait_ge(s_amax, w + 1)
                pool.partition_all_reduce(amax_all[:, w:w + 1], amax[:, w:w + 1], P,
                                          bass.bass_isa.ReduceOp.max).then_inc(s_amaxall, 1)

            def body(i, par, second, first):
                if is_block(i, 0):
                    pool.wait_ge(s_const, 1)
                    gather(0, 0)
                    weight_max(ACT_W)
                    inverse_sqrt(0, 0)
                    gather(1, 1)
                    for w in (REC_W, VAL_W, FFN_W):
                        weight_max(w)
                    inverse_sqrt(0, 1)
                    return
                more = not (is_block(i, NBLK - 1) or is_block(i, NBLK))
                if more:
                    pool.wait_ge(s_h1, 4 * i)
                    gather(i + 1, 1 - par)
                inverse_sqrt(1, i - 1)
                if more:
                    inverse_sqrt(0, i + 1)

            iterations(pool, body)

        @block.tensor
        def _(pe):
            def weight_transposes(w, natural):
                for k in range(W_BANKS[w]):
                    n = W_FIRST[w] + k
                    if n >= 2 * KT + 4:
                        pe.wait_ge(s_wlo, n - 3)
                    for c in range(KT):
                        ins = pe.transpose(w_bank(n)[:, c * P:(c + 1) * P], natural(c, k), ident[:, :])
                    ins.then_inc(s_wps, 1)

            def x_slice(par, part, kk, t0, n):
                src = xT[par][part][:, kk % KT, :, :]
                off = 1 if kk < KT else 2
                if t0 is None:
                    return src[:, :, off:off + SEQ]
                return src[:, t0 // SEQ, off + t0 % SEQ:off + t0 % SEQ + n]

            PARTS = ((0, 0), (0, 1), (1, 0))

            def body(i, par, second, first):
                if is_block(i, 0):
                    pe.wait_ge(s_idf, 2)
                    pe.wait_ge(s_idsf, 1)
                    pe.transpose(bank[7][:, 0:TOKENS // P], ids_f[:, :], ident[0:TOKENS // P, 0:TOKENS // P])\
                        .then_inc(s_idsT, 1)
                    pe.wait_ge(s_wdma[0], 16)
                    pe.wait_ge(s_rows, 1)
                    weight_transposes(ACT_W, lambda c, k: wact_n[:, c, k * P:(k + 1) * P])
                    pe.wait_ge(s_wlo, 4)
                if is_block(i, 1):
                    pe.wait_ge(s_wlo, W_ALL)
                if first:
                    for k in range(KT):
                        for t in range(TT):
                            if k == 0:
                                pe.wait_ge(s_xn, 4 * i + t + 1)
                            ins = pe.transpose(bank[k][:, t * P:(t + 1) * P],
                                               xn[:, t, k * P:(k + 1) * P], ident[:, :])
                        ins.then_inc(s_xps, 1)
                    if is_block(i, 0):
                        pe.wait_ge(s_wlo, 2 * KT)
                    pe.wait_ge(s_xhi, 4 * i + 4)
                    pe.wait_ge(s_xlo, 4 * i + 4)
                    for c in range(KT):
                        if is_block(i, 1):
                            pe.wait_ge(s_rsig, c + 1)
                        elif not is_block(i, 0):
                            pe.wait_ge(s_fin, 4 * i - 7 + c)
                        n = 0
                        for k in range(2 * KT):
                            for a, b in PARTS:
                                ins = pe.matmul(bank[4 + c][:, :].rearrange("p (s t) -> p s t", s=NSEQ),
                                                wact_t[a][:, k, c * P:(c + 1) * P],
                                                x_slice(par, b, k, None, 0),
                                                start=(n == 0), stop=(n == 6 * KT - 1))
                                n += 1
                        ins.then_inc(s_aps, 1)
                if second:
                    pe.wait_ge(s_kvhi, 2 * i)
                    pe.wait_ge(s_kvlo, 2 * i)
                    for t in range(TT):
                        n = 0
                        for k in range(KT):
                            for a, b in PARTS:
                                ins = pe.matmul(bank[t][:, :], kv[a][:, k // 2, k % 2, t * P:(t + 1) * P],
                                                wval_t[b][:, k, :], start=(n == 0), stop=(n == 3 * KT - 1))
                                n += 1
                        ins.then_inc(s_vps, 1)
                if is_block(i, 0):
                    pe.wait_ge(s_wdma[1], 16)
                    weight_transposes(REC_W, lambda c, k: wrec_n[:, c, k * P:(k + 1) * P])
                    pe.wait_ge(s_wlo, 4 * KT)
                if first:
                    for t in range(TT):
                        pe.wait_ge(s_z, 4 * i + t + 1)
                        n = 0
                        for k in range(2 * KT):
                            for a, b in PARTS:
                                ins = pe.matmul(bank[4 + t][:, :], x_slice(par, a, k, t * P, P),
                                                wrec_t[b][:, k, :], start=(n == 0), stop=(n == 6 * KT - 1))
                                n += 1
                        ins.then_inc(s_rps, 1)
                if is_block(i, 0):
                    pe.wait_ge(s_wdma[2], 16)
                    weight_transposes(VAL_W, lambda c, k: wval_n[:, c, (k // 2) * 2 * P + k % 2:(k // 2 + 1) * 2 * P:2])
                    pe.wait_ge(s_lvl, 4)
                    weight_transposes(FFN_W, lambda c, k: wvar_n[:, c * DIM + k * P:c * DIM + (k + 1) * P])
                    pe.wait_ge(s_id16, 1)
                if second:
                    for k in range(KT):
                        for t in range(TT):
                            if k == 0:
                                pe.wait_ge(s_q, 4 * i - 4 + t + 1)
                            dst = bank[k // 2][:, :].bitcast(F16)
                            ins = pe.transpose(dst[:, (k % 2) * BLOCK + t * P:(k % 2) * BLOCK + (t + 1) * P],
                                               q[:, t, k * P:(k + 1) * P], ident16[:, :])
                        if k % 2:
                            ins.then_inc(s_qps, 1)
                    for t in range(TT):
                        if first:
                            pe.wait_ge(s_rsig, 4 * i + t + 1)
                        elif t == 0:
                            pe.wait_ge(s_fin, 4 * i - 4)
                        if t == 0:
                            pe.wait_ge(s_qT, 2 * i)
                        n = 0
                        for k in range(KT):
                            for b in (0, 1):
                                ins = pe.matmul(bank[4 + t][:, :], qT[:, k, t * P:(t + 1) * P],
                                                wffn_t[b][:, k, :], start=(n == 0), stop=(n == 2 * KT - 1))
                                n += 1
                        ins.then_inc(s_fps, 1)

            iterations(pe, body)

        @block.scalar
        def _(act):
            def norm(n, i, par, src, dst, done, t):
                act.activation(dst[:, t, :], src[:, par, t, :], ACT.Identity,
                               bias=nbias[n][:, t:t + 1], scale=rstd[n][:, t:t + 1]).then_inc(done, 1)

            def weight_hi(w):
                act.wait_ge(s_sc, 4 * w + 4)
                for k in range(W_BANKS[w]):
                    n = W_FIRST[w] + k
                    act.wait_ge(s_wps, n + 1)
                    act.activation(W_DST[w][0][:, k, :], w_bank(n)[:, :], ACT.Identity,
                                   scale=wscale[:, w:w + 1]).then_inc(s_whi, 1)

            def xn_tiles(i, par):
                act.wait_ge(s_nb[0], i + 1)
                for t in range(TT):
                    norm(0, i, par, h, xn, s_xn, t)

            def body(i, par, second, first):
                if is_block(i, 0):
                    weight_hi(ACT_W)
                    xn_tiles(0, 0)
                if first:
                    for k in range(KT):
                        act.wait_ge(s_xps, 4 * i + k + 1)
                        act.activation(xT[par][0][:, k, :, 2:], bank[k][:, :].rearrange("p (s t) -> p s t", s=NSEQ),
                                       ACT.Copy).then_inc(s_xhi, 1)
                if second:
                    for p in range(PAIRS):
                        act.wait_ge(s_sd[p], SD * i)
                        act.activation(kv[0][:, p, :, :], z[:, p, :, :], ACT.Copy).then_inc(s_kvhi, 1)
                if first:
                    if second:
                        act.wait_ge(s_kvlo, 2 * i)
                    for p in range(PAIRS):
                        for c in range(2):
                            act.wait_ge(s_aps, 4 * i + 2 * p + c + 1)
                            act.activation(z[:, p, c, :], bank[4 + 2 * p + c][:, :], ACT.Sigmoid,
                                           scale=unscale[:, ACT_W:ACT_W + 1]).then_inc(s_z, 1)
                    for p in range(PAIRS):
                        act.wait_ge(s_sd[p], SD * i + 1)
                        act.activation(ab[:, p, :, :], z[:, p, :, :], ACT.Square).then_inc(s_sa[p], 1)
                    for p in range(PAIRS):
                        act.activation(cd[:, p, :, :], z[:, p, :, :], ACT.Ln).then_inc(s_sa[p], 1)
                    for p in range(PAIRS):
                        act.wait_ge(s_sd[p], SD * i + 2)
                        act.activation(ab[:, p, 0, :], ab[:, p, 0, :], ACT.Ln).then_inc(s_sa[p], 1)
                if is_block(i, 0):
                    weight_hi(REC_W)
                if second:
                    act.wait_ge(s_nb[1], i)
                    for t in range(TT):
                        norm(1, i - 1, 1 - par, h1, y, s_y, t)
                if first:
                    for p in range(PAIRS):
                        act.wait_ge(s_sd[p], SD * i + 3)
                        act.activation(cd[:, p, 0, :], cd[:, p, 0, :], ACT.Tanh, scale=0.5).then_inc(s_sa[p], 1)
                    for p in range(PAIRS):
                        act.wait_ge(s_sa[p], SA * i + 4)
                        act.activation(cd[:, p, 0, :], cd[:, p, 0, :], ACT.Arctan).then_inc(s_sa[p], 1)
                    for t in range(TT):
                        if t == 2 and not is_block(i, NBLK - 1):
                            xn_tiles(i + 1, 1 - par)
                        act.wait_ge(s_rps, 4 * i + t + 1)
                        act.activation(r4[:, t, :], bank[4 + t][:, :], ACT.Sigmoid,
                                       scale=unscale[:, REC_W:REC_W + 1]).then_inc(s_rsig, 1)
                if second:
                    for k in range(KT // 2):
                        act.wait_ge(s_qps, 2 * i - 2 + k + 1)
                        act.activation(qT[:, 2 * k:2 * k + 2, :].rearrange("p a b -> p (a b)"),
                                       bank[k][:, :].bitcast(F16), ACT.Copy).then_inc(s_qT, 1)
                if is_block(i, 0):
                    weight_hi(VAL_W)
                    weight_hi(FFN_W)
                if first:
                    act.wait_ge(s_rmax, i + 1)
                    act.activation(r4[:, :, :], r4[:, :, :], ACT.Square).then_inc(s_r2, 1)
                    for p in range(PAIRS):
                        act.wait_ge(s_sd[p], SD * i + 13)
                        act.activation(cd[:, p, 1, :], cd[:, p, 0, :], ACT.Abs).then_inc(s_sa[p], 1)
                    act.wait_ge(s_r2, i + 1)
                    act.activation(r4[:, :, :], r4[:, :, :], ACT.Square).then_inc(s_r4, 1)
                    for p in range(PAIRS):
                        act.activation(z[:, p, 1, :], cd[:, p, 0, :], ACT.Sin).then_inc(s_sa[p], 1)
                        act.wait_ge(s_sa[p], SA * i + 6)
                        act.activation(z[:, p, 0, :], cd[:, p, 1, :], ACT.Sin, bias=half_pi[:, :],
                                       scale=-1.0).then_inc(s_sa[p], 1)
                    for p in range(PAIRS):
                        act.wait_ge(s_sd[p], SD * i + 7)
                        act.activation(ab[:, p, 1, :], ab[:, p, 1, :], ACT.Exp, scale=0.5).then_inc(s_sa[p], 1)

            act.wait_ge(s_const, 2)
            iterations(act, body)

        @block.vector
        def _(dve):
            def scan(p, out_c, out_h, data0, data1, initial, op0, op1):
                for s in range(NSEQ):
                    cols = slice(s * SEQ, (s + 1) * SEQ)
                    dve.tensor_tensor_scan(out_c[:, p, out_h, cols], data0[:, cols],
                                           data1[:, cols] if data1 is not None else step_row[:, :],
                                           initial, op0, op1).then_inc(s_sd[p], 1)

            def norm_stats(n, i, par, src):
                for t in range(TT):
                    dve.bn_stats(stats[n][:, t, :], src[:, par, t, :]).then_inc(s_bn[n], 1)

            def norm_var(n, i, eps_scale):
                dve.wait_ge(s_bn[n], 4 * i + 4)
                dve.sem_inc(s_held[1], 1)
                for t in range(TT):
                    dve.bn_aggr(mv[n][:, t, :], stats[n][:, t, :]).then_inc(s_mv[n], 1)
                dve.wait_ge(s_mv[n], 4 * i + 4)
                dve.tensor_scalar(ve[n][:, :], mv[n][:, :, 1], EPS, eps_scale, ALU.add, ALU.mult)\
                    .then_inc(s_ve[n], 1)

            def norm_bias(n, i):
                dve.wait_ge(s_rstd[n], i + 1)
                dve.scalar_tensor_tensor(nbias[n][:, :], mv[n][:, :, 0], -1.0, rstd[n][:, :],
                                         ALU.mult, ALU.mult).then_inc(s_nb[n], 1)

            def weight_scale(w):
                one = slice(w, w + 1)
                dve.wait_ge(s_amaxall, w + 1)
                dve.tensor_scalar(amax_pos[:, one], amax_all[:, one], 1e-30, None, ALU.max).then_inc(s_sc, 1)
                dve.wait_ge(s_sc, 4 * w + 1)
                dve.tensor_scalar(pow2[:, one].bitcast(I32), amax_pos[:, one].bitcast(I32), EXP_MASK, None,
                                  ALU.bitwise_and).then_inc(s_sc, 1)
                dve.wait_ge(s_sc, 4 * w + 2)
                dve.tensor_scalar(wscale[:, one].bitcast(I32), pow2[:, one].bitcast(I32), -1.0,
                                  float((2 * 127 + W_EXP) << 23), ALU.mult, ALU.add).then_inc(s_sc, 1)
                dve.tensor_scalar(unscale[:, one], pow2[:, one], UNSCALE[w], None, ALU.mult).then_inc(s_sc, 1)
                dve.wait_ge(s_sc, 4 * w + 4)

            def weight_lo(w):
                for k in range(W_BANKS[w]):
                    n = W_FIRST[w] + k
                    dve.wait_ge(s_whi, n + 1)
                    dve.scalar_tensor_tensor(W_DST[w][1][:, k, :], w_bank(n)[:, :], wscale[:, w:w + 1],
                                             W_DST[w][0][:, k, :], ALU.mult, ALU.subtract).then_inc(s_wlo, 1)

            def weight_amax(w, src):
                dve.tensor_reduce(amax[:, w:w + 1], src, AX.X, ALU.max,
                                  apply_absolute_value=True).then_inc(s_amax, 1)

            def product_start(p, i):
                dve.wait_ge(s_z, 4 * i + 2 * p + 2)
                dve.tensor_scalar(z[:, p, :, :], z[:, p, :, :], 0.5, None, ALU.max).then_inc(s_sd[p], 1)

            def product_square(p, i):
                dve.wait_ge(s_sa[p], SA * i + 1)
                dve.tensor_tensor(ab[:, p, 0, :], ab[:, p, 0, :], ab[:, p, 1, :], ALU.add).then_inc(s_sd[p], 1)

            def product_modulus(p, i):
                dve.wait_ge(s_sa[p], SA * i + 2)
                dve.tensor_tensor(cd[:, p, 0, :], cd[:, p, 1, :], cd[:, p, 0, :], ALU.subtract)\
                    .then_inc(s_sd[p], 1)
                dve.wait_ge(s_sa[p], SA * i + 3)
                scan(p, ab, 1, ab[:, p, 0, :], ab[:, p, 0, :], -1e30, ALU.max, ALU.max)
                dve.wait_ge(s_sd[p], SD * i + 5)
                scan(p, ab, 1, ab[:, p, 0, :], ab[:, p, 1, :], 0.0, ALU.add, ALU.subtract)

            def product_angle(i):
                for p in range(PAIRS):
                    dve.wait_ge(s_sa[p], SA * i + 5)
                    scan(p, cd, 1, cd[:, p, 0, :], None, 0.0, ALU.add, ALU.add)
                for p in range(PAIRS):
                    dve.wait_ge(s_sd[p], SD * i + 9)
                    dve.tensor_scalar(cd[:, p, 0, :], cd[:, p, 1, :], 1 / TWO_PI, MAGIC, ALU.mult, ALU.add)\
                        .then_inc(s_sd[p], 1)
                for p in range(PAIRS):
                    dve.wait_ge(s_sd[p], SD * i + 10)
                    dve.tensor_scalar(cd[:, p, 0, :], cd[:, p, 0, :], MAGIC, -TWO_PI, ALU.subtract, ALU.mult)\
                        .then_inc(s_sd[p], 1)
                for p in range(PAIRS):
                    dve.wait_ge(s_sd[p], SD * i + 11)
                    dve.tensor_tensor(cd[:, p, 0, :], cd[:, p, 0, :], cd[:, p, 1, :], ALU.add)\
                        .then_inc(s_sd[p], 1)
                for p in range(PAIRS):
                    dve.wait_ge(s_sd[p], SD * i + 12)
                    dve.tensor_scalar(cd[:, p, 0, :], cd[:, p, 0, :], PI_IN, -PI_IN, ALU.min, ALU.max)\
                        .then_inc(s_sd[p], 1)

            def body(i, par, second, first):
                more = not (is_block(i, NBLK - 1) or is_block(i, NBLK))
                if is_block(i, 0):
                    dve.memset(half_pi[:, :], HALF_PI).then_inc(s_const, 1)
                    for b in range(2):
                        for part in range(2):
                            dve.memset(xT[b][part][:, :, :, 0:2], 0.0).then_inc(s_pad, 1)
                    dve.wait_ge(s_ids, 16)
                    dve.tensor_copy(ids_f[:, :], ids_i[:, :]).then_inc(s_idsf, 1)
                    dve.wait_ge(s_idsT, 1)
                    dve.tensor_scalar(over[:, :], bank[7][:, 0:TOKENS // P], float(VOCAB - EXTRA), float(EXTRA),
                                      ALU.is_ge, ALU.mult).then_inc(s_over, 1)
                    dve.wait_ge(s_over, 1)
                    dve.tensor_tensor(rows[:, :], bank[7][:, 0:TOKENS // P], over[:, :], ALU.add)\
                        .then_inc(s_rows, 1)
                    dve.wait_ge(s_wdma[0], 16)
                    weight_amax(ACT_W, w_stage[:, :])
                    weight_scale(ACT_W)
                    dve.wait_ge(s_gath, 64)
                    norm_stats(0, 0, 0, h)
                    norm_var(0, 0, X_SCALE ** -2)
                    norm_bias(0, 0)
                    weight_lo(ACT_W)
                if first:
                    for k in range(KT):
                        dve.wait_ge(s_xhi, 4 * i + k + 1)
                        dve.tensor_tensor(xT[par][1][:, k, :, 2:],
                                          bank[k][:, :].rearrange("p (s t) -> p s t", s=NSEQ),
                                          xT[par][0][:, k, :, 2:], ALU.subtract).then_inc(s_xlo, 1)
                if is_block(i, 0):
                    dve.wait_ge(s_wdma[1], 16)
                    weight_amax(REC_W, h1[:, :, :, :].rearrange("p a t n -> p (a t n)"))
                    weight_scale(REC_W)
                if second:
                    for p in range(PAIRS):
                        dve.wait_ge(s_sa[p], SA * i)
                        for c in range(2):
                            ins = dve.scalar_tensor_tensor(z[:, p, c, :], ab[:, p, 1, :], KV_SCALE, z[:, p, c, :],
                                                           ALU.mult, ALU.mult)
                        ins.then_inc(s_sd[p], 1)
                    for p in range(PAIRS):
                        dve.wait_ge(s_kvhi, 2 * i - 2 + p + 1)
                        dve.tensor_tensor(kv[1][:, p, :, :], z[:, p, :, :], kv[0][:, p, :, :], ALU.subtract)\
                            .then_inc(s_kvlo, 1)
                if first:
                    for p in range(PAIRS):
                        product_start(p, i)
                    for p in range(PAIRS):
                        product_square(p, i)
                if is_block(i, 0):
                    weight_lo(REC_W)
                if first:
                    product_modulus(0, i)
                if second:
                    if not (is_block(i, 1) or is_block(i, 2)):
                        dve.wait_ge(s_out[1 - par], 8 * i - (8 if par else 16))
                    dve.wait_ge(s_r4, i)
                    for t in range(TT):
                        dve.wait_ge(s_vps, 4 * i - 4 + t + 1)
                        dve.scalar_tensor_tensor(h1[:, 1 - par, t, :], bank[t][:, :], unscale[:, VAL_W:VAL_W + 1],
                                                 r4[:, t, :], ALU.mult, ALU.mult).then_inc(s_t, 1)
                        dve.wait_ge(s_t, 4 * i - 4 + t + 1)
                        dve.tensor_tensor(h1[:, 1 - par, t, :], h1[:, 1 - par, t, :], h[:, 1 - par, t, :], ALU.add)\
                            .then_inc(s_h1, 1)
                        dve.wait_ge(s_h1, 4 * i - 4 + t + 1)
                        dve.bn_stats(stats[1][:, t, :], h1[:, 1 - par, t, :]).then_inc(s_bn[1], 1)
                    norm_var(1, i - 1, 1.0)
                    norm_bias(1, i - 1)
                if first:
                    product_modulus(1, i)
                if second:
                    for t in range(TT):
                        dve.wait_ge(s_y, 4 * i - 4 + t + 1)
                        dve.tensor_scalar(below[:, t, :], y[:, t, :], -X_THRESHOLD, None, ALU.is_lt)\
                            .then_inc(s_below, 1)
                        dve.wait_ge(s_below, 4 * i - 4 + t + 1)
                        dve.scalar_tensor_tensor(q[:, t, :], y[:, t, :], X_THRESHOLD, below[:, t, :],
                                                 ALU.is_gt, ALU.subtract).then_inc(s_q, 1)
                if is_block(i, 0):
                    dve.wait_ge(s_wdma[3], 16)
                    dve.wait_ge(s_wdma[4], 16)
                    dve.tensor_scalar(level[:, :], wffn_n, W_THRESHOLD, W_LEVEL, ALU.is_gt, ALU.mult)\
                        .then_inc(s_lvl, 1)
                    dve.wait_ge(s_lvl, 1)
                    dve.tensor_tensor(wvar_n, wvar_n, level[:, :], ALU.add).then_inc(s_lvl, 1)
                    dve.wait_ge(s_lvl, 2)
                    dve.tensor_scalar(level[:, :], wffn_n, -W_THRESHOLD, -W_LEVEL, ALU.is_lt, ALU.mult)\
                        .then_inc(s_lvl, 1)
                    dve.wait_ge(s_lvl, 3)
                    dve.tensor_tensor(wvar_n, wvar_n, level[:, :], ALU.add).then_inc(s_lvl, 1)
                    dve.wait_ge(s_wdma[2], 16)
                    weight_amax(VAL_W, w_stage[:, 0:2048])
                    dve.wait_ge(s_lvl, 4)
                    weight_amax(FFN_W, wvar_n)
                    weight_scale(VAL_W)
                    weight_scale(FFN_W)
                if first and more:
                    dve.wait_ge(s_gath, 64 * i + 128)
                    norm_stats(0, i + 1, 1 - par, h)
                    norm_var(0, i + 1, X_SCALE ** -2)
                    norm_bias(0, i + 1)
                if first:
                    if is_block(i, 0):
                        dve.wait_ge(s_steps, 16)
                    product_angle(i)
                    dve.wait_ge(s_rsig, 4 * i + 4)
                    dve.tensor_scalar(r4[:, :, :], r4[:, :, :], 0.5, None, ALU.max).then_inc(s_rmax, 1)
                if is_block(i, 0):
                    weight_lo(VAL_W)
                    weight_lo(FFN_W)
                if second:
                    for t in range(TT):
                        dve.wait_ge(s_fps, 4 * i - 4 + t + 1)
                        dve.scalar_tensor_tensor(h1[:, 1 - par, t, :], bank[4 + t][:, :], unscale[:, FFN_W:FFN_W + 1],
                                                 h1[:, 1 - par, t, :], ALU.mult, ALU.add).then_inc(s_fin, 1)

            iterations(dve, body)


def kernel(x, L0_tok_weight, L0_tok_extra, L0_attn_W_act, L0_attn_W_val, L0_attn_W_rec, L0_ffn_weight,
           L0_ffn_rram_variation):
    import concourse.bacc as bacc
    from concourse.bass_utils import run_bass_kernel_spmd

    arrays = {
        "ids": np.ascontiguousarray(x),
        "table": np.concatenate([np.asarray(L0_tok_weight), np.asarray(L0_tok_extra)], axis=0),
        "w_act": np.ascontiguousarray(L0_attn_W_act),
        "w_val": np.ascontiguousarray(L0_attn_W_val),
        "w_rec": np.ascontiguousarray(L0_attn_W_rec),
        "w_ffn": np.ascontiguousarray(L0_ffn_weight),
        "w_var": np.ascontiguousarray(L0_ffn_rram_variation),
        "steps": np.ascontiguousarray(np.broadcast_to(phase_steps(), (P, SEQ))),
    }
    nc = bacc.Bacc("TRN2", target_bir_lowering=False, num_devices=1)
    args = [nc.dram_tensor(name, a.shape, mybir.dt.from_np(a.dtype), kind="ExternalInput").ap()
            for name, a in arrays.items()]
    out = nc.dram_tensor("out", (BATCH, SEQ, DIM), F32, kind="ExternalOutput").ap()
    tower_kernel(nc, *args, out)
    result = run_bass_kernel_spmd(nc, [arrays], core_ids=[0])
    return result.results[0]["out"]
```

```python
from contextlib import ExitStack

import numpy as np

import concourse.bass as bass
from concourse import mybir

ALU = mybir.AluOpType
ACT = mybir.ActivationFunctionType
AX = mybir.AxisListType
F32 = mybir.dt.float32
F16 = mybir.dt.float16
I32 = mybir.dt.int32

P = 128
BATCH, SEQ, DIM, VOCAB, EXTRA = 32, 256, 512, 32000, 4
TOKENS = BATCH * SEQ
BLOCK = 512
NBLK = TOKENS // BLOCK
NSEQ = BLOCK // SEQ
TT = BLOCK // P
KT = DIM // P
PAIRS = KT // 2
SEQ_COLS = SEQ + 2

EPS = 1e-5
X_SCALE = 256.0
KV_SCALE = 2.0 ** 14
W_EXP = 13
EXP_MASK = 0x7F800000
MAGIC = 1.5 * 2.0 ** 23
TWO_PI = float(np.float32(2 * np.pi))
HALF_PI = float(np.float32(np.pi / 2))
PI_IN = 3.1415925
X_THRESHOLD, W_THRESHOLD, W_LEVEL = 0.33, 0.2, 0.6

SD, SA = 14, 9


def is_block(i, n):
    return isinstance(i, int) and i == n


def phase_steps():
    steps, total = np.zeros(SEQ, np.float32), 0.0
    for t in range(SEQ):
        want = ((t + 1) % 8) * np.pi / 4
        if want > np.pi:
            want -= 2 * np.pi
        steps[t] = np.float32(want - total)
        total += float(steps[t])
    return steps


def tower_kernel(nc, x, table, w_act, w_val, w_rec, w_ffn, w_var, steps, out):
    with ExitStack() as ctx:
        def sb(name, shape, dt=F32):
            return ctx.enter_context(nc.sbuf_tensor(name, shape, dt))

        def sem(name):
            return ctx.enter_context(nc.semaphore(name))

        bank = [ctx.enter_context(nc.psum_tensor(f"bank{b}", [P, 512], F32)) for b in range(8)]

        ident = sb("ident", [P, P])
        ident16 = sb("ident16", [P, P], F16)
        step_row = sb("step_row", [P, SEQ])
        half = sb("half", [P, TT])
        half_pi = sb("half_pi", [P, 1])
        wact_t = [sb(f"wact_{n}", [P, 2 * KT, DIM], F16) for n in ("hi", "lo")]
        wrec_t = [sb(f"wrec_{n}", [P, 2 * KT, DIM], F16) for n in ("hi", "lo")]
        wval_t = [sb(f"wval_{n}", [P, KT, DIM], F16) for n in ("hi", "lo")]
        wffn_t = [sb(f"wffn_{n}", [P, KT, DIM], F16) for n in ("hi", "lo")]
        ids_i = sb("ids_i", [TOKENS // P, P], I32)
        ids_f = sb("ids_f", [TOKENS // P, P])
        over = sb("over", [P, TOKENS // P])
        rows = sb("rows", [P, TOKENS // P], I32)
        rows_now = sb("rows_now", [P, 2, TT], I32)
        h = sb("h", [P, 2, TT, DIM])
        h1 = sb("h1", [P, 2, TT, DIM])
        xn = sb("xn", [P, TT, DIM])
        xT = [[sb(f"xT_{n}{b}", [P, KT, NSEQ, SEQ_COLS], F16) for n in ("hi", "lo")] for b in range(2)]
        z = sb("z", [P, PAIRS, 2, BLOCK])
        ab = sb("ab", [P, PAIRS, 2, BLOCK])
        cd = sb("cd", [P, PAIRS, 2, BLOCK])
        kv = [sb(f"kv_{n}", [P, PAIRS, 2, BLOCK], F16) for n in ("hi", "lo")]
        r4 = sb("r4", [P, TT, DIM])
        y = sb("y", [P, TT, DIM])
        below = sb("below", [P, TT, DIM], F16)
        q = sb("q", [P, TT, DIM], F16)
        qT = sb("qT", [P, KT, BLOCK], F16)
        stats = [sb(f"stats{n}", [P, TT, 6]) for n in (1, 2)]
        mv = [sb(f"mv{n}", [P, TT, 2]) for n in (1, 2)]
        ve = [sb(f"ve{n}", [P, TT]) for n in (1, 2)]
        rstd = [sb(f"rstd{n}", [P, TT]) for n in (1, 2)]
        nbias = [sb(f"nbias{n}", [P, TT]) for n in (1, 2)]
        w_stage = sb("w_stage", [P, 4096])
        wact_n = w_stage[:, :].rearrange("p (c k) -> p c k", c=KT)
        wrec_n = h1[:, :, :, :].rearrange("p a t n -> p (a t n)").rearrange("p (c k) -> p c k", c=KT)
        wval_n = w_stage[:, 0:2048].rearrange("p (c k) -> p c k", c=KT)
        wffn_n = w_stage[:, 2048:4096]
        wvar_n = y[:, :, :].rearrange("p c k -> p (c k)")
        level_t = sb("level", [P, 2048])
        level = level_t[:, :]
        NW = 4
        chunk_max = sb("chunk_max", [P, KT])
        amax = sb("amax", [P, NW])
        amax_all = sb("amax_all", [P, NW])
        amax_pos = sb("amax_pos", [P, NW])
        pow2 = sb("pow2", [P, NW])
        wscale = sb("wscale", [P, NW])
        unscale = sb("unscale", [P, NW])
        UNSCALE = [2.0 ** -W_EXP / X_SCALE, 2.0 ** -W_EXP / X_SCALE,
                   2.0 ** -W_EXP / KV_SCALE, 2.0 ** -W_EXP * 0.5]

        s_wact = [sem(f"s_wact_loaded{c}") for c in range(KT)]
        s_wdma = [None] + [sem(f"s_wdma_{n}") for n in ("rec", "val", "ffn", "var")]
        s_chunk = sem("s_wact_chunk_max")
        s_ids, s_steps = sem("s_ids_loaded"), sem("s_steps_loaded")
        s_const = sem("s_constants")
        s_idsf, s_idsT, s_over, s_rows = sem("s_ids_float"), sem("s_ids_T"), sem("s_over"), sem("s_rows")
        s_idf, s_id16 = sem("s_ident"), sem("s_ident16")
        s_pad = sem("s_xT_zero_cols")
        s_amax, s_amaxall = sem("s_amax"), sem("s_amax_all")
        s_sc = sem("s_scale_steps")
        s_lvl = sem("s_ffn_levels")
        s_wps, s_whi, s_wlo = sem("s_w_transposed"), sem("s_w_hi"), sem("s_w_lo")
        s_now, s_kept = sem("s_rows_now"), sem("s_rows_kept")
        s_gath = [sem(f"s_gathered{b}") for b in range(2)]
        s_bn = [sem(f"s_bn{n}") for n in (1, 2)]
        s_held = [sem(f"s_wait_carrier_{e}") for e in ("pool", "dve")]
        s_mv = [sem(f"s_mv{n}") for n in (1, 2)]
        s_ve = [sem(f"s_ve{n}") for n in (1, 2)]
        s_rstd = [sem(f"s_rstd{n}") for n in (1, 2)]
        s_nb = [sem(f"s_nbias{n}") for n in (1, 2)]
        s_xn = sem("s_xn")
        s_xps, s_xhi, s_xlo = sem("s_x_transposed"), sem("s_xT_hi"), sem("s_xT_lo")
        s_aps, s_z = sem("s_act_product"), sem("s_z")
        s_sd = [sem(f"s_scan_dve{p}") for p in range(PAIRS)]
        s_sa = [sem(f"s_scan_act{p}") for p in range(PAIRS)]
        s_kvhi, s_kvlo = sem("s_kv_hi"), sem("s_kv_lo")
        s_vps, s_t, s_h1 = sem("s_val_product"), sem("s_val_gated"), sem("s_h1")
        s_y, s_below, s_q = sem("s_y"), sem("s_below"), sem("s_q")
        s_qps, s_qT = sem("s_q_transposed"), sem("s_qT")
        s_rps, s_rsig, s_rmax = sem("s_rec_product"), sem("s_r_sigmoid"), sem("s_r_max")
        s_r2, s_r4 = sem("s_r2"), sem("s_r4")
        s_fps, s_fin = sem("s_ffn_product"), sem("s_final")
        s_out = [sem(f"s_stored{b}") for b in range(2)]

        out_v = out.rearrange("b s d -> (b s) d")
        ACT_W, REC_W, VAL_W, FFN_W = range(NW)
        W_FIRST = {ACT_W: 0, REC_W: 2 * KT, VAL_W: 4 * KT, FFN_W: 5 * KT}
        W_BANKS = {ACT_W: 2 * KT, REC_W: 2 * KT, VAL_W: KT, FFN_W: KT}
        W_DST = {ACT_W: wact_t, REC_W: wrec_t, VAL_W: wval_t, FFN_W: wffn_t}
        W_ALL = 6 * KT

        def w_bank(n):
            return bank[n] if n < 2 * KT else bank[n % 4]

        block = ctx.enter_context(nc.Block())

        def iterations(engine, body):
            body(0, 0)
            body(1, 1)
            with engine.Fori(2, NBLK - 3, 2) as i:
                body(i, 2)
                body(i + 1, 3)
            for n in range(NBLK - 2, NBLK + 1):
                body(n, n)

        def halves(i):
            return (not is_block(i, NBLK), not is_block(i, 0),
                    not is_block(i, NBLK) and not is_block(i, NBLK - 1))

        @block.sync
        def _(sp):
            sp.dma_start(ids_i[:, :], x.rearrange("b (a p) -> (b a) p", p=P)).then_inc(s_ids, 16)
            w_act_v = w_act.rearrange("(r p two) k -> r two p k", p=P, two=2)
            for c in range(KT):
                sp.dma_start(wact_n[:, c, :], w_act_v[c // 2, c % 2, :, :]).then_inc(s_wact[c], 16)
            sp.dma_start(step_row[:, :], steps[:, :]).then_inc(s_steps, 16)
            sp.wait_ge(s_gath[0], 64)
            sp.dma_start(wrec_n, w_rec.rearrange("(c p) k -> p c k", p=P)).then_inc(s_wdma[1], 16)
            sp.dma_start(wvar_n.rearrange("p (c k) -> p c k", c=KT),
                         w_var.rearrange("(c p) k -> p c k", p=P)).then_inc(s_wdma[4], 16)
            sp.wait_ge(s_wps, 2 * KT)
            sp.wait_ge(s_chunk, KT)
            sp.dma_start(wffn_n.rearrange("p (c k) -> p c k", c=KT),
                         w_ffn.rearrange("(c p) k -> p c k", p=P)).then_inc(s_wdma[3], 16)
            sp.dma_start(wval_n, w_val.rearrange("(c p) k -> p c k", p=P)).then_inc(s_wdma[2], 16)

            def store(i, n):
                if is_block(i, 0):
                    return
                old = (n - 1) % 2
                rows_v = out_v[bass.ds((i - 1) * BLOCK, BLOCK), :].rearrange("(t p) d -> p t d", p=P)
                if is_block(i, NBLK):
                    for t in range(TT):
                        sp.wait_ge(s_fin, 4 * i - 4 + t + 1)
                        sp.dma_start(rows_v[:, t, :], h1[:, old, t, :]).then_inc(s_out[old], 16)
                    return
                sp.wait_ge(s_fin, 4 * i)
                sp.dma_start(rows_v, h1[:, old, :, :]).then_inc(s_out[old], 16)

            iterations(sp, store)
            for b in range(2):
                sp.wait_ge(s_out[b], 8 * NBLK + 16 * (TT - 1) * b)

        @block.gpsimd
        def _(pool):
            pool.memset(ident[:, :], 0.0).then_inc(s_idf, 1)
            pool.memset(half[:, :], -0.5).then_inc(s_const, 1)
            pool.wait_ge(s_idf, 1)
            pool.affine_select(out=ident[:, :], in_=ident[:, :], compare_op=ALU.not_equal, fill=1.0,
                               base=0, pattern=[[-1, P]], channel_multiplier=1).then_inc(s_idf, 1)
            pool.wait_ge(s_idf, 2)
            pool.tensor_copy(ident16[:, :], ident[:, :]).then_inc(s_id16, 1)

            def gather(i, slot):
                pool.tensor_copy(rows_now[:, slot, :], rows[:, bass.ds(i * TT, TT)]).then_inc(s_now, 1)
                pool.wait_ge(s_now, i + 1)
                pool.sem_inc(s_held[0], 1)
                for t in range(TT):
                    pool.indirect_dma_start(
                        h[:, slot, t, :], None, table,
                        bass.IndirectOffsetOnAxis(ap=rows_now[:, slot, t:t + 1], axis=0),
                    ).then_inc(s_gath[slot], 16)

            def inverse_sqrt(n, i):
                pool.wait_ge(s_ve[n], i + 1)
                pool.tensor_tensor(rstd[n][:, :], ve[n][:, :], half[:, :], ALU.pow).then_inc(s_rstd[n], 1)

            def weight_max(w):
                pool.wait_ge(s_amax, w + 1)
                pool.partition_all_reduce(amax_all[:, w:w + 1], amax[:, w:w + 1], P,
                                          bass.bass_isa.ReduceOp.max).then_inc(s_amaxall, 1)

            def body(i, n):
                first, second, more = halves(i)
                if is_block(i, 0):
                    pool.wait_ge(s_const, 1)
                    pool.wait_ge(s_rows, 1)
                    gather(0, 0)
                    weight_max(ACT_W)
                    inverse_sqrt(0, 0)
                    gather(1, 1)
                    for w in (REC_W, VAL_W, FFN_W):
                        weight_max(w)
                    inverse_sqrt(0, 1)
                elif more:
                    inverse_sqrt(0, i + 1)
                if more and not is_block(i, NBLK - 2):
                    pool.wait_ge(s_kept, i + 1)
                    gather(i + 2, n % 2)
                if second:
                    inverse_sqrt(1, i - 1)

            iterations(pool, body)

        @block.tensor
        def _(pe):
            def weight_transposes(w, ks, natural):
                for k in ks:
                    n = W_FIRST[w] + k
                    if 3 * KT <= n < 5 * KT:
                        pe.wait_ge(s_wlo, n - 3)
                    for c in range(KT):
                        ins = pe.transpose(w_bank(n)[:, c * P:(c + 1) * P], natural(c, k), ident[:, :])
                    ins.then_inc(s_wps, 1)

            def x_slice(par, part, kk, t0, n):
                src = xT[par][part][:, kk % KT, :, :]
                off = 1 if kk < KT else 2
                if t0 is None:
                    return src[:, :, off:off + SEQ]
                return src[:, t0 // SEQ, off + t0 % SEQ:off + t0 % SEQ + n]

            PARTS = ((0, 0), (0, 1), (1, 0))

            def x_transposes(i):
                for k in range(KT):
                    for t in range(TT):
                        if k == 0:
                            pe.wait_ge(s_xn, 4 * i + t + 1)
                        ins = pe.transpose(bank[k][:, t * P:(t + 1) * P],
                                           xn[:, t, k * P:(k + 1) * P], ident[:, :])
                    ins.then_inc(s_xps, 1)

            def act_product(i, par, c):
                n = 0
                for k in range(2 * KT):
                    for a, b in PARTS:
                        ins = pe.matmul(bank[4 + c][:, :].rearrange("p (s t) -> p s t", s=NSEQ),
                                        wact_t[a][:, k, c * P:(c + 1) * P], x_slice(par, b, k, None, 0),
                                        start=(n == 0), stop=(n == 6 * KT - 1))
                        n += 1
                ins.then_inc(s_aps, 1)

            def val_product(t):
                n = 0
                for k in range(KT):
                    for a, b in PARTS:
                        ins = pe.matmul(bank[t][:, :], kv[a][:, k // 2, k % 2, t * P:(t + 1) * P],
                                        wval_t[b][:, k, :], start=(n == 0), stop=(n == 3 * KT - 1))
                        n += 1
                ins.then_inc(s_vps, 1)

            def rec_product(par, t):
                n = 0
                for k in range(2 * KT):
                    for a, b in PARTS:
                        ins = pe.matmul(bank[4 + t][:, :], x_slice(par, a, k, t * P, P),
                                        wrec_t[b][:, k, :], start=(n == 0), stop=(n == 6 * KT - 1))
                        n += 1
                ins.then_inc(s_rps, 1)

            def q_transposes(i):
                for k in range(KT):
                    dst = bank[k // 2][:, :].bitcast(F16)
                    for t in range(TT):
                        if k == 0:
                            pe.wait_ge(s_q, 4 * i + t + 1)
                        ins = pe.transpose(dst[:, (k % 2) * BLOCK + t * P:(k % 2) * BLOCK + (t + 1) * P],
                                           q[:, t, k * P:(k + 1) * P], ident16[:, :])
                    if k % 2:
                        ins.then_inc(s_qps, 1)

            def ffn_product(t):
                n = 0
                for k in range(KT):
                    for b in (0, 1):
                        ins = pe.matmul(bank[4 + t][:, :], qT[:, k, t * P:(t + 1) * P],
                                        wffn_t[b][:, k, :], start=(n == 0), stop=(n == 2 * KT - 1))
                        n += 1
                ins.then_inc(s_fps, 1)

            rec_natural = lambda c, k: wrec_n[:, c, k * P:(k + 1) * P]

            def body(i, n):
                first, second, more = halves(i)
                start = is_block(i, 0)
                par = n % 2
                if start:
                    pe.wait_ge(s_idf, 2)
                    pe.wait_ge(s_idsf, 1)
                    pe.transpose(bank[7][:, 0:TOKENS // P], ids_f[:, :], ident[0:TOKENS // P, 0:TOKENS // P])\
                        .then_inc(s_idsT, 1)
                    for c in range(KT):
                        pe.wait_ge(s_wact[c], 16)
                    pe.wait_ge(s_rows, 1)
                    weight_transposes(ACT_W, range(2 * KT), lambda c, k: wact_n[:, c, k * P:(k + 1) * P])
                    pe.wait_ge(s_wlo, 4)
                    x_transposes(0)
                    pe.wait_ge(s_wlo, 2 * KT)
                if first:
                    pe.wait_ge(s_xhi, 4 * i + 4)
                    pe.wait_ge(s_xlo, 4 * i + 4)
                    for c in range(KT):
                        if is_block(i, 1):
                            pe.wait_ge(s_rsig, c + 1)
                        elif not start:
                            pe.wait_ge(s_fin, 4 * i - 7 + c)
                        act_product(i, par, c)
                        if start and c == 0:
                            pe.wait_ge(s_wdma[1], 16)
                        if start and c < 2:
                            weight_transposes(REC_W, range(KT * c, KT * c + KT), rec_natural)
                if second:
                    pe.wait_ge(s_kvhi, 2 * i)
                    pe.wait_ge(s_kvlo, 2 * i)
                    if is_block(i, 1):
                        pe.wait_ge(s_wlo, W_ALL)
                    for t in range(TT):
                        val_product(t)
                if start:
                    pe.wait_ge(s_wlo, 4 * KT)
                if first:
                    for t in range(TT):
                        pe.wait_ge(s_z, 4 * i + t + 1)
                        rec_product(par, t)
                        if start and t == 0:
                            pe.wait_ge(s_wdma[2], 16)
                            weight_transposes(VAL_W, range(KT), lambda c, k: wval_n[
                                :, c, (k // 2) * 2 * P + k % 2:(k // 2 + 1) * 2 * P:2])
                        if t == 1 and more:
                            if start:
                                pe.wait_ge(s_wlo, 5 * KT)
                            else:
                                pe.wait_ge(s_t, 4 * i)
                            x_transposes(i + 1)
                        if t == 2:
                            if more:
                                pe.wait_ge(s_xhi, 4 * i + 8)
                                pe.wait_ge(s_xlo, 4 * i + 8)
                            if start:
                                pe.wait_ge(s_lvl, 4)
                                weight_transposes(FFN_W, range(KT), lambda c, k: wvar_n[
                                    :, c * DIM + k * P:c * DIM + (k + 1) * P])
                                pe.wait_ge(s_id16, 1)
                            else:
                                q_transposes(i - 1)
                if second:
                    if not first:
                        q_transposes(i - 1)
                        pe.wait_ge(s_fin, 4 * i - 4)
                    for t in range(TT):
                        if first:
                            pe.wait_ge(s_rsig, 4 * i + t + 1)
                        if t == 0:
                            pe.wait_ge(s_qT, 2 * i)
                        ffn_product(t)

            iterations(pe, body)

        @block.scalar
        def _(act):
            def norm(n, slot, src, dst, done, t):
                act.activation(dst[:, t, :], src[:, slot, t, :], ACT.Identity,
                               bias=nbias[n][:, t:t + 1], scale=rstd[n][:, t:t + 1]).then_inc(done, 1)

            def weight_hi(w, ks):
                if ks[0] == 0:
                    act.wait_ge(s_sc, 4 * w + 4)
                for k in ks:
                    n = W_FIRST[w] + k
                    act.wait_ge(s_wps, n + 1)
                    act.activation(W_DST[w][0][:, k, :], w_bank(n)[:, :], ACT.Identity,
                                   scale=wscale[:, w:w + 1]).then_inc(s_whi, 1)

            def xn_tiles(i, n):
                act.wait_ge(s_nb[0], i + 1)
                for t in range(TT):
                    norm(0, n % 2, h, xn, s_xn, t)

            def xT_hi(i, n):
                for k in range(KT):
                    act.wait_ge(s_xps, 4 * i + k + 1)
                    act.activation(xT[n % 2][0][:, k, :, 2:], bank[k][:, :].rearrange("p (s t) -> p s t", s=NSEQ),
                                   ACT.Copy).then_inc(s_xhi, 1)

            def keep_rows(i, n):
                if not is_block(i, 0) and not is_block(i, 1):
                    act.wait_ge(s_out[n % 2], 8 * i - 8 * (n % 2))
                act.activation(h1[:, n % 2, :, :], h[:, n % 2, :, :], ACT.Copy).then_inc(s_kept, 1)

            def body(i, n):
                first, second, more = halves(i)
                start = is_block(i, 0)
                if start:
                    weight_hi(ACT_W, range(2 * KT))
                    xn_tiles(0, 0)
                    xT_hi(0, 0)
                if first:
                    if second:
                        act.wait_ge(s_kvlo, 2 * i)
                    for p in range(PAIRS):
                        for c in range(2):
                            act.wait_ge(s_aps, 4 * i + 2 * p + c + 1)
                            act.activation(z[:, p, c, :], bank[4 + 2 * p + c][:, :], ACT.Sigmoid,
                                           scale=unscale[:, ACT_W:ACT_W + 1]).then_inc(s_z, 1)
                            if start and p == 0:
                                weight_hi(REC_W, range(KT * c, KT * c + KT))
                            if not start and p == 0 and c == 0:
                                keep_rows(i, n)
                        if p == 0:
                            act.wait_ge(s_sd[p], SD * i + 1)
                            act.activation(ab[:, p, :, :], z[:, p, :, :], ACT.Square).then_inc(s_sa[p], 1)
                    if start:
                        keep_rows(i, n)
                    act.wait_ge(s_sd[1], SD * i + 1)
                    act.activation(ab[:, 1, :, :], z[:, 1, :, :], ACT.Square).then_inc(s_sa[1], 1)
                    for p in range(PAIRS):
                        act.activation(cd[:, p, :, :], z[:, p, :, :], ACT.Ln).then_inc(s_sa[p], 1)
                        act.wait_ge(s_sd[p], SD * i + 2)
                        act.activation(ab[:, p, 0, :], ab[:, p, 0, :], ACT.Ln).then_inc(s_sa[p], 1)
                if more:
                    xn_tiles(i + 1, n + 1)
                if first:
                    for p in range(PAIRS):
                        act.wait_ge(s_sd[p], SD * i + 3)
                        act.activation(cd[:, p, 0, :], cd[:, p, 0, :], ACT.Tanh, scale=0.5).then_inc(s_sa[p], 1)
                    for p in range(PAIRS):
                        act.wait_ge(s_sd[p], SD * i + 7)
                        act.activation(ab[:, p, 1, :], ab[:, p, 1, :], ACT.Exp, scale=0.5).then_inc(s_sa[p], 1)
                if second:
                    act.wait_ge(s_nb[1], i)
                    for t in range(TT):
                        norm(1, (n - 1) % 2, h1, y, s_y, t)
                if first:
                    for p in range(PAIRS):
                        act.wait_ge(s_sa[p], SA * i + 4)
                        act.activation(cd[:, p, 0, :], cd[:, p, 0, :], ACT.Arctan).then_inc(s_sa[p], 1)
                    for t in range(TT):
                        act.wait_ge(s_rps, 4 * i + t + 1)
                        act.activation(r4[:, t, :], bank[4 + t][:, :], ACT.Sigmoid,
                                       scale=unscale[:, REC_W:REC_W + 1]).then_inc(s_rsig, 1)
                        if start and t == 0:
                            weight_hi(VAL_W, range(KT))
                        if t == 1 and more:
                            xT_hi(i + 1, n + 1)
                        if t == 2 and start:
                            weight_hi(FFN_W, range(KT))
                        if t == 2 and second:
                            q_copies(i)
                    for p in range(PAIRS):
                        act.wait_ge(s_sd[p], SD * i + 13)
                        act.activation(cd[:, p, 1, :], cd[:, p, 0, :], ACT.Abs).then_inc(s_sa[p], 1)
                    act.wait_ge(s_rmax, i + 1)
                    act.activation(r4[:, :, :], r4[:, :, :], ACT.Square).then_inc(s_r2, 1)
                    for p in range(PAIRS):
                        act.activation(z[:, p, 1, :], cd[:, p, 0, :], ACT.Sin).then_inc(s_sa[p], 1)
                        act.wait_ge(s_sa[p], SA * i + 7)
                        act.activation(z[:, p, 0, :], cd[:, p, 1, :], ACT.Sin, bias=half_pi[:, :],
                                       scale=-1.0).then_inc(s_sa[p], 1)
                    act.wait_ge(s_r2, i + 1)
                    act.activation(r4[:, :, :], r4[:, :, :], ACT.Square).then_inc(s_r4, 1)
                    for p in range(PAIRS):
                        act.wait_ge(s_sd[p], SD * i + SD)
                        act.activation(kv[0][:, p, :, :], z[:, p, :, :], ACT.Copy).then_inc(s_kvhi, 1)
                elif second:
                    q_copies(i)

            def q_copies(i):
                for k in range(KT // 2):
                    act.wait_ge(s_qps, 2 * i - 2 + k + 1)
                    act.activation(qT[:, 2 * k:2 * k + 2, :].rearrange("p a b -> p (a b)"),
                                   bank[k][:, :].bitcast(F16), ACT.Copy).then_inc(s_qT, 1)

            act.wait_ge(s_const, 2)
            iterations(act, body)

        @block.vector
        def _(dve):
            def scan(p, out_c, out_h, data0, data1, initial, op0, op1):
                for s in range(NSEQ):
                    cols = slice(s * SEQ, (s + 1) * SEQ)
                    dve.tensor_tensor_scan(out_c[:, p, out_h, cols], data0[:, cols],
                                           data1[:, cols] if data1 is not None else step_row[:, :],
                                           initial, op0, op1).then_inc(s_sd[p], 1)

            def norm_stats(n, slot, src):
                for t in range(TT):
                    dve.bn_stats(stats[n][:, t, :], src[:, slot, t, :]).then_inc(s_bn[n], 1)

            def norm_var(n, i, eps_scale):
                dve.wait_ge(s_bn[n], 4 * i + 4)
                dve.sem_inc(s_held[1], 1)
                for t in range(TT):
                    dve.bn_aggr(mv[n][:, t, :], stats[n][:, t, :]).then_inc(s_mv[n], 1)
                dve.wait_ge(s_mv[n], 4 * i + 4)
                dve.tensor_scalar(ve[n][:, :], mv[n][:, :, 1], EPS, eps_scale, ALU.add, ALU.mult)\
                    .then_inc(s_ve[n], 1)

            def norm_bias(n, i):
                dve.wait_ge(s_rstd[n], i + 1)
                dve.scalar_tensor_tensor(nbias[n][:, :], mv[n][:, :, 0], -1.0, rstd[n][:, :],
                                         ALU.mult, ALU.mult).then_inc(s_nb[n], 1)

            def weight_scale(w):
                one = slice(w, w + 1)
                dve.wait_ge(s_amaxall, w + 1)
                dve.tensor_scalar(amax_pos[:, one], amax_all[:, one], 1e-30, None, ALU.max).then_inc(s_sc, 1)
                dve.wait_ge(s_sc, 4 * w + 1)
                dve.tensor_scalar(pow2[:, one].bitcast(I32), amax_pos[:, one].bitcast(I32), EXP_MASK, None,
                                  ALU.bitwise_and).then_inc(s_sc, 1)
                dve.wait_ge(s_sc, 4 * w + 2)
                dve.tensor_scalar(wscale[:, one].bitcast(I32), pow2[:, one].bitcast(I32), -1.0,
                                  float((2 * 127 + W_EXP) << 23), ALU.mult, ALU.add).then_inc(s_sc, 1)
                dve.tensor_scalar(unscale[:, one], pow2[:, one], UNSCALE[w], None, ALU.mult).then_inc(s_sc, 1)
                dve.wait_ge(s_sc, 4 * w + 4)

            def weight_lo(w, ks):
                for k in ks:
                    n = W_FIRST[w] + k
                    dve.wait_ge(s_whi, n + 1)
                    dve.scalar_tensor_tensor(W_DST[w][1][:, k, :], w_bank(n)[:, :], wscale[:, w:w + 1],
                                             W_DST[w][0][:, k, :], ALU.mult, ALU.subtract).then_inc(s_wlo, 1)

            def largest(dst, src, done):
                dve.tensor_reduce(dst, src, AX.X, ALU.max, apply_absolute_value=True).then_inc(done, 1)

            def xT_lo(i, n):
                for k in range(KT):
                    dve.wait_ge(s_xhi, 4 * i + k + 1)
                    dve.tensor_tensor(xT[n % 2][1][:, k, :, 2:], bank[k][:, :].rearrange("p (s t) -> p s t", s=NSEQ),
                                      xT[n % 2][0][:, k, :, 2:], ALU.subtract).then_inc(s_xlo, 1)

            def clamp_z(p, i):
                dve.wait_ge(s_z, 4 * i + 2 * p + 2)
                dve.tensor_scalar(z[:, p, :, :], z[:, p, :, :], 0.5, None, ALU.max).then_inc(s_sd[p], 1)

            def square_z(p, i):
                dve.wait_ge(s_sa[p], SA * i + 1)
                dve.tensor_tensor(ab[:, p, 0, :], ab[:, p, 0, :], ab[:, p, 1, :], ALU.add).then_inc(s_sd[p], 1)

            def product_modulus(p, i):
                dve.wait_ge(s_sa[p], SA * i + 2)
                dve.tensor_tensor(cd[:, p, 0, :], cd[:, p, 1, :], cd[:, p, 0, :], ALU.subtract)\
                    .then_inc(s_sd[p], 1)
                dve.wait_ge(s_sa[p], SA * i + 3)
                scan(p, ab, 1, ab[:, p, 0, :], ab[:, p, 0, :], -1e30, ALU.max, ALU.max)
                dve.wait_ge(s_sd[p], SD * i + 5)
                scan(p, ab, 1, ab[:, p, 0, :], ab[:, p, 1, :], 0.0, ALU.add, ALU.subtract)

            def product_angle(i):
                for p in range(PAIRS):
                    dve.wait_ge(s_sa[p], SA * i + 6)
                    scan(p, cd, 1, cd[:, p, 0, :], None, 0.0, ALU.add, ALU.add)
                for p in range(PAIRS):
                    dve.wait_ge(s_sd[p], SD * i + 9)
                    dve.tensor_scalar(cd[:, p, 0, :], cd[:, p, 1, :], 1 / TWO_PI, MAGIC, ALU.mult, ALU.add)\
                        .then_inc(s_sd[p], 1)
                for p in range(PAIRS):
                    dve.wait_ge(s_sd[p], SD * i + 10)
                    dve.tensor_scalar(cd[:, p, 0, :], cd[:, p, 0, :], MAGIC, -TWO_PI, ALU.subtract, ALU.mult)\
                        .then_inc(s_sd[p], 1)
                for p in range(PAIRS):
                    dve.wait_ge(s_sd[p], SD * i + 11)
                    dve.tensor_tensor(cd[:, p, 0, :], cd[:, p, 0, :], cd[:, p, 1, :], ALU.add)\
                        .then_inc(s_sd[p], 1)
                for p in range(PAIRS):
                    dve.wait_ge(s_sd[p], SD * i + 12)
                    dve.tensor_scalar(cd[:, p, 0, :], cd[:, p, 0, :], PI_IN, -PI_IN, ALU.min, ALU.max)\
                        .then_inc(s_sd[p], 1)

            def product_parts(i):
                for p in range(PAIRS):
                    dve.wait_ge(s_sa[p], SA * i + SA)
                    for c in range(2):
                        ins = dve.scalar_tensor_tensor(z[:, p, c, :], ab[:, p, 1, :], KV_SCALE, z[:, p, c, :],
                                                       ALU.mult, ALU.mult)
                    ins.then_inc(s_sd[p], 1)
                for p in range(PAIRS):
                    dve.wait_ge(s_kvhi, 2 * i + p + 1)
                    dve.tensor_tensor(kv[1][:, p, :, :], z[:, p, :, :], kv[0][:, p, :, :], ALU.subtract)\
                        .then_inc(s_kvlo, 1)

            def ffn_levels():
                dve.wait_ge(s_wdma[3], 16)
                dve.wait_ge(s_wdma[4], 16)
                dve.tensor_scalar(level, wffn_n, W_THRESHOLD, W_LEVEL, ALU.is_gt, ALU.mult).then_inc(s_lvl, 1)
                dve.wait_ge(s_lvl, 1)
                dve.tensor_tensor(wvar_n, wvar_n, level, ALU.add).then_inc(s_lvl, 1)
                dve.wait_ge(s_lvl, 2)
                dve.tensor_scalar(level, wffn_n, -W_THRESHOLD, -W_LEVEL, ALU.is_lt, ALU.mult).then_inc(s_lvl, 1)
                dve.wait_ge(s_lvl, 3)
                dve.tensor_tensor(wvar_n, wvar_n, level, ALU.add).then_inc(s_lvl, 1)

            def load_start():
                dve.memset(half_pi[:, :], HALF_PI).then_inc(s_const, 1)
                for b in range(2):
                    for part in range(2):
                        dve.memset(xT[b][part][:, :, :, 0:2], 0.0).then_inc(s_pad, 1)
                dve.wait_ge(s_ids, 16)
                dve.tensor_copy(ids_f[:, :], ids_i[:, :]).then_inc(s_idsf, 1)
                dve.wait_ge(s_idsT, 1)
                dve.tensor_scalar(over[:, :], bank[7][:, 0:TOKENS // P], float(VOCAB - EXTRA), float(EXTRA),
                                  ALU.is_ge, ALU.mult).then_inc(s_over, 1)
                dve.wait_ge(s_over, 1)
                dve.tensor_tensor(rows[:, :], bank[7][:, 0:TOKENS // P], over[:, :], ALU.add)\
                    .then_inc(s_rows, 1)
                for c in range(KT):
                    dve.wait_ge(s_wact[c], 16)
                    largest(chunk_max[:, c:c + 1], wact_n[:, c, :], s_chunk)
                dve.wait_ge(s_chunk, KT)
                largest(amax[:, 0:1], chunk_max[:, :], s_amax)
                weight_scale(ACT_W)
                weight_lo(ACT_W, range(4))
                dve.wait_ge(s_gath[0], 64)
                norm_stats(0, 0, h)
                norm_var(0, 0, X_SCALE ** -2)
                weight_lo(ACT_W, range(4, 6))
                norm_bias(0, 0)
                weight_lo(ACT_W, range(6, 8))
                xT_lo(0, 0)
                dve.wait_ge(s_wdma[1], 16)
                largest(amax[:, REC_W:REC_W + 1], h1[:, :, :, :].rearrange("p a t n -> p (a t n)"), s_amax)
                weight_scale(REC_W)

            def body(i, n):
                first, second, more = halves(i)
                start = is_block(i, 0)
                old = (n - 1) % 2
                if start:
                    load_start()
                    weight_lo(REC_W, range(KT))
                elif more:
                    dve.wait_ge(s_gath[(n + 1) % 2], 32 * i + (96 if n % 2 else 64))
                    norm_stats(0, (n + 1) % 2, h)
                    norm_var(0, i + 1, X_SCALE ** -2)
                    norm_bias(0, i + 1)
                if first:
                    clamp_z(0, i)
                    square_z(0, i)
                if start:
                    weight_lo(REC_W, range(KT, 2 * KT))
                    ffn_levels()
                if first:
                    clamp_z(1, i)
                    square_z(1, i)
                if start:
                    dve.wait_ge(s_wdma[2], 16)
                    largest(amax[:, VAL_W:VAL_W + 1], w_stage[:, 0:2048], s_amax)
                    dve.wait_ge(s_lvl, 4)
                    largest(amax[:, FFN_W:FFN_W + 1], wvar_n, s_amax)
                    weight_scale(VAL_W)
                    weight_scale(FFN_W)
                    dve.wait_ge(s_gath[1], 64)
                    norm_stats(0, 1, h)
                    norm_var(0, 1, X_SCALE ** -2)
                    norm_bias(0, 1)
                if first:
                    product_modulus(0, i)
                    product_modulus(1, i)
                if start:
                    weight_lo(VAL_W, range(KT))
                if second:
                    dve.wait_ge(s_r4, i)
                    dve.wait_ge(s_kept, i)
                    for t in range(TT):
                        dve.wait_ge(s_vps, 4 * i - 4 + t + 1)
                        dve.scalar_tensor_tensor(r4[:, t, :], bank[t][:, :], unscale[:, VAL_W:VAL_W + 1],
                                                 r4[:, t, :], ALU.mult, ALU.mult).then_inc(s_t, 1)
                        dve.wait_ge(s_t, 4 * i - 4 + t + 1)
                        dve.tensor_tensor(h1[:, old, t, :], h1[:, old, t, :], r4[:, t, :], ALU.add)\
                            .then_inc(s_h1, 1)
                        dve.wait_ge(s_h1, 4 * i - 4 + t + 1)
                        dve.bn_stats(stats[1][:, t, :], h1[:, old, t, :]).then_inc(s_bn[1], 1)
                    norm_var(1, i - 1, 1.0)
                    norm_bias(1, i - 1)
                    for t in range(TT):
                        dve.wait_ge(s_y, 4 * i - 4 + t + 1)
                        dve.tensor_scalar(below[:, t, :], y[:, t, :], -X_THRESHOLD, None, ALU.is_lt)\
                            .then_inc(s_below, 1)
                        dve.wait_ge(s_below, 4 * i - 4 + t + 1)
                        dve.scalar_tensor_tensor(q[:, t, :], y[:, t, :], X_THRESHOLD, below[:, t, :],
                                                 ALU.is_gt, ALU.subtract).then_inc(s_q, 1)
                if more:
                    xT_lo(i + 1, n + 1)
                if start:
                    dve.wait_ge(s_steps, 16)
                if first:
                    product_angle(i)
                if start:
                    weight_lo(FFN_W, range(KT))
                if first:
                    dve.wait_ge(s_rsig, 4 * i + 4)
                    dve.tensor_scalar(r4[:, :, :], r4[:, :, :], 0.5, None, ALU.max).then_inc(s_rmax, 1)
                if second:
                    for t in range(TT):
                        dve.wait_ge(s_fps, 4 * i - 4 + t + 1)
                        dve.scalar_tensor_tensor(h1[:, old, t, :], bank[4 + t][:, :], unscale[:, FFN_W:FFN_W + 1],
                                                 h1[:, old, t, :], ALU.mult, ALU.add).then_inc(s_fin, 1)
                if first:
                    product_parts(i)

            iterations(dve, body)


def kernel(x, L0_tok_weight, L0_tok_extra, L0_attn_W_act, L0_attn_W_val, L0_attn_W_rec, L0_ffn_weight,
           L0_ffn_rram_variation):
    import concourse.bacc as bacc
    from concourse.bass_utils import run_bass_kernel_spmd

    arrays = {
        "ids": np.ascontiguousarray(x),
        "table": np.concatenate([np.asarray(L0_tok_weight), np.asarray(L0_tok_extra)], axis=0),
        "w_act": np.ascontiguousarray(L0_attn_W_act),
        "w_val": np.ascontiguousarray(L0_attn_W_val),
        "w_rec": np.ascontiguousarray(L0_attn_W_rec),
        "w_ffn": np.ascontiguousarray(L0_ffn_weight),
        "w_var": np.ascontiguousarray(L0_ffn_rram_variation),
        "steps": np.ascontiguousarray(np.broadcast_to(phase_steps(), (P, SEQ))),
    }
    nc = bacc.Bacc("TRN2", target_bir_lowering=False, num_devices=1)
    args = [nc.dram_tensor(name, a.shape, mybir.dt.from_np(a.dtype), kind="ExternalInput").ap()
            for name, a in arrays.items()]
    out = nc.dram_tensor("out", (BATCH, SEQ, DIM), F32, kind="ExternalOutput").ap()
    tower_kernel(nc, *args, out)
    result = run_bass_kernel_spmd(nc, [arrays], core_ids=[0])
    return result.results[0]["out"]
```

```python
from contextlib import ExitStack

import numpy as np

import concourse.bass as bass
from concourse import mybir

ALU = mybir.AluOpType
ACT = mybir.ActivationFunctionType
AX = mybir.AxisListType
F32 = mybir.dt.float32
F16 = mybir.dt.float16
I32 = mybir.dt.int32

P = 128
BATCH, SEQ, DIM, VOCAB, EXTRA = 32, 256, 512, 32000, 4
TOKENS = BATCH * SEQ
BLOCK = 512
NBLK = TOKENS // BLOCK
NSEQ = BLOCK // SEQ
TT = BLOCK // P
KT = DIM // P
PAIRS = KT // 2
SEQ_PAD = 16
SEQ_COLS = SEQ_PAD + SEQ

EPS = 1e-5
X_SCALE = 256.0
KV_SCALE = 2.0 ** 14
W_EXP = 13
EXP_MASK = 0x7F800000
MAGIC = 1.5 * 2.0 ** 23
TWO_PI = float(np.float32(2 * np.pi))
HALF_PI = float(np.float32(np.pi / 2))
PI_IN = 3.1415925
X_THRESHOLD, W_THRESHOLD, W_LEVEL = 0.33, 0.2, 0.6

SD, SA = 14, 9


def is_block(i, n):
    return isinstance(i, int) and i == n


def phase_steps():
    steps, total = np.zeros(SEQ, np.float32), 0.0
    for t in range(SEQ):
        want = ((t + 1) % 8) * np.pi / 4
        if want > np.pi:
            want -= 2 * np.pi
        steps[t] = np.float32(want - total)
        total += float(steps[t])
    return steps


def tower_kernel(nc, x, table, w_act, w_val, w_rec, w_ffn, w_var, steps, out):
    with ExitStack() as ctx:
        def sb(name, shape, dt=F32):
            return ctx.enter_context(nc.sbuf_tensor(name, shape, dt))

        def sem(name):
            return ctx.enter_context(nc.semaphore(name))

        bank = [ctx.enter_context(nc.psum_tensor(f"bank{b}", [P, 512], F32)) for b in range(8)]

        ident = sb("ident", [P, P])
        step_row = sb("step_row", [P, SEQ])
        half = sb("half", [P, TT])
        half_pi = sb("half_pi", [P, 1])
        wact_t = [sb(f"wact_{n}", [P, KT, 2 * KT, P], F16) for n in ("hi", "lo")]
        wrec_t = [sb(f"wrec_{n}", [P, KT, 2 * KT, P], F16) for n in ("hi", "lo")]
        wval_t = [sb(f"wval_{n}", [P, KT, KT, P], F16) for n in ("hi", "lo")]
        wffn_t = [sb(f"wffn_{n}", [P, KT, KT, P], F16) for n in ("hi", "lo")]
        ids_i = sb("ids_i", [TOKENS // P, P], I32)
        ids_f = sb("ids_f", [TOKENS // P, P])
        over = sb("over", [P, TOKENS // P])
        rows = sb("rows", [P, TOKENS // P], I32)
        rows_now = sb("rows_now", [P, 2, TT], I32)
        h = sb("h", [P, 2, TT, DIM])
        h1 = sb("h1", [P, 2, TT, DIM])
        xn = sb("xn", [P, TT, DIM])
        xn16 = [sb(f"xn_{n}", [P, TT, DIM], F16) for n in ("hi", "lo")]
        TILE_AT = [s * (SEQ // P) + j for j in range(SEQ // P) for s in range(NSEQ)]
        xT = [[sb(f"xT_{n}{b}", [P, NSEQ, KT, SEQ_COLS], F16) for n in ("hi", "lo")] for b in range(2)]
        z = sb("z", [P, PAIRS, 2, BLOCK])
        ab = sb("ab", [P, PAIRS, 2, BLOCK])
        cd = sb("cd", [P, PAIRS, 2, BLOCK])
        kv = [sb(f"kv_{n}", [P, PAIRS, 2, BLOCK], F16) for n in ("hi", "lo")]
        r4 = sb("r4", [P, TT, DIM])
        y = sb("y", [P, TT, DIM])
        below = sb("below", [P, TT, DIM], F16)
        q = sb("q", [P, TT, DIM], F16)
        qT = sb("qT", [P, TT, KT, P], F16)
        stats = [sb(f"stats{n}", [P, TT, 6]) for n in (1, 2)]
        mv = [sb(f"mv{n}", [P, TT, 2]) for n in (1, 2)]
        ve = [sb(f"ve{n}", [P, TT]) for n in (1, 2)]
        rstd = [sb(f"rstd{n}", [P, TT]) for n in (1, 2)]
        nbias = [sb(f"nbias{n}", [P, TT]) for n in (1, 2)]
        w_stage = sb("w_stage", [P, 4096])
        wact_n = w_stage[:, :].rearrange("p (c k) -> p c k", c=KT)
        wrec_n = h1[:, :, :, :].rearrange("p a t n -> p (a t n)").rearrange("p (c k) -> p c k", c=KT)
        wval_n = w_stage[:, 0:2048].rearrange("p (c k) -> p c k", c=KT)
        wffn_n = w_stage[:, 2048:4096]
        wvar_n = y[:, :, :].rearrange("p c k -> p (c k)")
        level = xn[:, :, :].rearrange("p c k -> p (c k)")
        ACT_W, REC_W, VAL_W, FFN_W = range(4)
        W_DST = {ACT_W: wact_t, REC_W: wrec_t, VAL_W: wval_t, FFN_W: wffn_t}

        def natural(w, c):
            if w == ACT_W:
                return wact_n[:, c, :]
            if w == REC_W:
                return wrec_n[:, c, :]
            if w == VAL_W:
                return wval_n[:, c, :].rearrange("p (r q two) -> p r two q", r=PAIRS, two=2)
            return wvar_n[:, c * DIM:(c + 1) * DIM]

        def parts(w, c, n, a):
            if w == ACT_W:
                flat = r4[:, :, :] if a == 0 else cd[:, :, :, :].rearrange("p a b c -> p (a b) c")
                return flat.rearrange("p a b -> p (a b)")[:, c * DIM:(c + n) * DIM].bitcast(F16)
            if w == REC_W:
                if a == 0:
                    flat = (q, below)[c // 2][:, :, :].rearrange("p a b -> p (a b)")
                else:
                    flat = kv[c // 2][:, :, :, :].rearrange("p a b c -> p (a b c)")
                return flat[:, (c % 2) * 2 * DIM:(c % 2 + n) * 2 * DIM]
            if w == VAL_W:
                flat = (q, below)[a][:, :, :].rearrange("p a b -> p (a b)")
            elif a == 0:
                flat = qT[:, :, :, :].rearrange("p a b c -> p (a b c)")
            else:
                flat = wffn_n.bitcast(F16)
            return flat[:, c * DIM:(c + n) * DIM]

        NS = KT + 3
        SCALE_COL = {ACT_W: 0, REC_W: KT, VAL_W: KT + 1, FFN_W: KT + 2}
        chunk_max = sb("chunk_max", [P, KT])
        amax = sb("amax", [P, NS])
        amax_all = sb("amax_all", [P, NS])
        amax_pos = sb("amax_pos", [P, NS])
        pow2 = sb("pow2", [P, NS])
        wscale = sb("wscale", [P, NS])
        unscale = sb("unscale", [P, NS])
        UNSCALE = [2.0 ** -W_EXP / X_SCALE] * (KT + 1) + [2.0 ** -W_EXP / KV_SCALE, 2.0 ** -W_EXP * 0.5]

        def column(w, c=0):
            first = SCALE_COL[w] + (c if w == ACT_W else 0)
            return slice(first, first + 1)

        s_wact = [sem(f"s_wact_loaded{c}") for c in range(KT)]
        s_wrec = [sem(f"s_wrec_loaded{c}") for c in range(KT)]
        s_wval, s_wffn, s_wvar = sem("s_wval_loaded"), sem("s_wffn_loaded"), sem("s_wvar_loaded")
        s_rowmax, s_chunk = sem("s_wact_row_max"), sem("s_wrec_chunk_max")
        s_ids, s_steps = sem("s_ids_loaded"), sem("s_steps_loaded")
        s_const = sem("s_constants")
        s_idsf, s_idsT, s_over, s_rows = sem("s_ids_float"), sem("s_ids_T"), sem("s_over"), sem("s_rows")
        s_idf = sem("s_ident")
        s_pad = sem("s_xT_zero_cols")
        s_amax, s_amaxall = sem("s_amax"), sem("s_amax_all")
        s_sc = sem("s_scale_steps")
        s_lvl = sem("s_ffn_levels")
        s_whi, s_wlo = sem("s_w_hi"), sem("s_w_lo")
        s_wactT = [sem(f"s_wact_transposed{c}") for c in range(KT)]
        s_wrecT = [sem(f"s_wrec_{n}_transposed") for n in ("hi", "lo")]
        s_wT = [None, None] + [sem(f"s_w{n}_transposed") for n in ("val", "ffn")]
        s_now, s_kept = sem("s_rows_now"), sem("s_rows_kept")
        s_first_rows = [sem(f"s_first_rows{t}") for t in range(TT)]
        s_gath = [sem(f"s_gathered{b}") for b in range(2)]
        s_bn = [sem(f"s_bn{n}") for n in (1, 2)]
        s_held = [sem(f"s_wait_carrier_{e}") for e in ("pool", "dve", "sp")]
        s_mv = [sem(f"s_mv{n}") for n in (1, 2)]
        s_ve = [sem(f"s_ve{n}") for n in (1, 2)]
        s_rstd = [sem(f"s_rstd{n}") for n in (1, 2)]
        s_nb = [sem(f"s_nbias{n}") for n in (1, 2)]
        s_xn, s_xhi, s_xlo = sem("s_xn"), sem("s_xn_hi"), sem("s_xn_lo")
        s_xT = [[sem(f"s_x_{n}_transposed{b}") for n in ("hi", "lo")] for b in range(2)]
        s_aps, s_z = sem("s_act_product"), sem("s_z")
        s_sd = [sem(f"s_scan_dve{p}") for p in range(PAIRS)]
        s_sa = [sem(f"s_scan_act{p}") for p in range(PAIRS)]
        s_kvhi, s_kvlo = sem("s_kv_hi"), sem("s_kv_lo")
        s_vps, s_t, s_h1 = sem("s_val_product"), sem("s_val_gated"), sem("s_h1")
        s_y, s_below, s_q = sem("s_y"), sem("s_below"), sem("s_q")
        s_qT = [sem(f"s_q_transposed{t}") for t in range(TT)]
        s_rps, s_rsig, s_rmax = sem("s_rec_product"), sem("s_r_sigmoid"), sem("s_r_max")
        s_r2, s_r4 = sem("s_r2"), sem("s_r4")
        s_fps, s_fin = sem("s_ffn_product"), sem("s_final")
        s_out = [sem(f"s_stored{b}") for b in range(2)]

        out_v = out.rearrange("b s d -> (b s) d")
        block = ctx.enter_context(nc.Block())

        def iterations(engine, body):
            body(0, 0)
            body(1, 1)
            with engine.Fori(2, NBLK - 3, 2) as i:
                body(i, 2)
                body(i + 1, 3)
            for n in range(NBLK - 2, NBLK + 1):
                body(n, n)

        def halves(i):
            return (not is_block(i, NBLK), not is_block(i, 0),
                    not is_block(i, NBLK) and not is_block(i, NBLK - 1))

        GROUPS = (slice(0, TT - 1), slice(TT - 1, TT))

        @block.sync
        def _(sp):
            sp.dma_start(ids_i[:, :], x.rearrange("b (a p) -> (b a) p", p=P)).then_inc(s_ids, 16)
            w_act_v = w_act.rearrange("(r p two) k -> r two p k", p=P, two=2)

            def load_act(c):
                sp.dma_start(wact_n[:, c, :], w_act_v[c // 2, c % 2, :, :]).then_inc(s_wact[c], 16)

            def load_rec(c):
                sp.dma_start(wrec_n[:, c, :], w_rec[c * P:(c + 1) * P, :]).then_inc(s_wrec[c], 16)

            def weight_transposes(w, c, n, done, which=(0, 1)):
                for a in which:
                    sp.wait_ge((s_whi, s_wlo)[a], KT * w + c + n)
                    sp.dma_start_transpose(
                        W_DST[w][a][:, c:c + n, :, :].rearrange("p c k x -> p (c k) x"),
                        parts(w, c, n, a)).then_inc(done, 16)

            def x_transposes(i, n):
                for split, a in ((s_xhi, 0), (s_xlo, 1)):
                    for j in range(SEQ // P):
                        sp.wait_ge(split, 4 * i + NSEQ * (j + 1))
                        sp.sem_inc(s_held[2], 1)
                        sp.dma_start_transpose(
                            xT[n % 2][a][:, :, :, SEQ_PAD + j * P:SEQ_PAD + (j + 1) * P]
                            .rearrange("p s k t -> p (s k) t"),
                            xn16[a][:, NSEQ * j:NSEQ * (j + 1), :].rearrange("p s c -> p (s c)"),
                        ).then_inc(s_xT[n % 2][a], 16)

            def q_transposes(i):
                for t in range(TT):
                    sp.wait_ge(s_q, 4 * i + t + 1)
                    sp.sem_inc(s_held[2], 1)
                    sp.dma_start_transpose(qT[:, t, :, :], q[:, t, :]).then_inc(s_qT[t], 16)

            def store(i, n):
                old = (n - 1) % 2
                rows_v = out_v[bass.ds((i - 1) * BLOCK, BLOCK), :].rearrange("(t p) d -> p t d", p=P)
                if is_block(i, NBLK):
                    for t in range(TT):
                        sp.wait_ge(s_fin, 4 * i - 4 + t + 1)
                        sp.dma_start(rows_v[:, t, :], h1[:, old, t, :]).then_inc(s_out[old], 16)
                    return
                sp.wait_ge(s_fin, 4 * i)
                sp.dma_start(rows_v, h1[:, old, :, :]).then_inc(s_out[old], 16)

            def load_start():
                load_act(0)
                load_act(1)
                for t in range(TT):
                    sp.wait_ge(s_first_rows[t], 16)
                load_act(2)
                load_act(3)
                weight_transposes(ACT_W, 0, 1, s_wactT[0])
                x_transposes(0, 0)
                weight_transposes(ACT_W, 1, 1, s_wactT[1])
                for c in range(KT):
                    load_rec(c)
                weight_transposes(ACT_W, 2, 1, s_wactT[2])
                weight_transposes(ACT_W, 3, 1, s_wactT[3])
                for a in range(2):
                    weight_transposes(REC_W, 0, 2, s_wrecT[a], (a,))
                    weight_transposes(REC_W, 2, 2, s_wrecT[a], (a,))

            def body(i, n):
                first, second, more = halves(i)
                if is_block(i, 0):
                    load_start()
                if more:
                    x_transposes(i + 1, n + 1)
                if is_block(i, 0):
                    sp.dma_start(wval_n, w_val.rearrange("(c p) k -> p c k", p=P)).then_inc(s_wval, 16)
                    sp.dma_start(wffn_n.rearrange("p (c k) -> p c k", c=KT),
                                 w_ffn.rearrange("(c p) k -> p c k", p=P)).then_inc(s_wffn, 16)
                    sp.dma_start(wvar_n.rearrange("p (c k) -> p c k", c=KT),
                                 w_var.rearrange("(c p) k -> p c k", p=P)).then_inc(s_wvar, 16)
                    sp.dma_start(step_row[:, :], steps[:, :]).then_inc(s_steps, 16)
                    weight_transposes(VAL_W, 0, KT, s_wT[VAL_W])
                if is_block(i, 1):
                    weight_transposes(FFN_W, 0, KT, s_wT[FFN_W])
                    sp.wait_ge(s_wT[FFN_W], 32)
                if second:
                    q_transposes(i - 1)
                    store(i, n)

            iterations(sp, body)
            for b in range(2):
                sp.wait_ge(s_out[b], 8 * NBLK + 16 * (TT - 1) * b)

        @block.gpsimd
        def _(pool):
            pool.memset(ident[:, :], 0.0).then_inc(s_idf, 1)
            pool.memset(half[:, :], -0.5).then_inc(s_const, 1)
            pool.wait_ge(s_idf, 1)
            pool.affine_select(out=ident[:, :], in_=ident[:, :], compare_op=ALU.not_equal, fill=1.0,
                               base=0, pattern=[[-1, P]], channel_multiplier=1).then_inc(s_idf, 1)

            def gather(i, slot):
                pool.tensor_copy(rows_now[:, slot, :], rows[:, bass.ds(i * TT, TT)]).then_inc(s_now, 1)
                pool.wait_ge(s_now, i + 1)
                pool.sem_inc(s_held[0], 1)
                for t in range(TT):
                    pool.indirect_dma_start(
                        h[:, slot, t, :], None, table,
                        bass.IndirectOffsetOnAxis(ap=rows_now[:, slot, t:t + 1], axis=0),
                    ).then_inc(s_first_rows[t] if is_block(i, 0) else s_gath[slot], 16)

            def inverse_sqrt(n, i):
                pool.wait_ge(s_ve[n], i + 1)
                pool.tensor_tensor(rstd[n][:, :], ve[n][:, :], half[:, :], ALU.pow).then_inc(s_rstd[n], 1)

            def weight_max(w):
                pool.wait_ge(s_amax, w)
                pool.partition_all_reduce(amax_all[:, column(w)], amax[:, column(w)], P,
                                          bass.bass_isa.ReduceOp.max).then_inc(s_amaxall, 1)

            def ffn_weights():
                pool.wait_ge(s_wvar, 16)
                pool.wait_ge(s_lvl, 2)
                pool.tensor_tensor(level, wffn_n, level, ALU.add).then_inc(s_lvl, 1)
                pool.wait_ge(s_lvl, 3)
                pool.tensor_tensor(wvar_n, wvar_n, level, ALU.add).then_inc(s_lvl, 1)

            def body(i, n):
                first, second, more = halves(i)
                if is_block(i, 0):
                    pool.wait_ge(s_const, 1)
                    pool.wait_ge(s_rows, 1)
                    gather(0, 0)
                    inverse_sqrt(0, 0)
                    weight_max(REC_W)
                    gather(1, 1)
                    inverse_sqrt(0, 1)
                    weight_max(VAL_W)
                    ffn_weights()
                elif more:
                    inverse_sqrt(0, i + 1)
                if more and not is_block(i, NBLK - 2):
                    pool.wait_ge(s_kept, i + 1)
                    gather(i + 2, n % 2)
                if is_block(i, 0):
                    weight_max(FFN_W)
                if is_block(i, NBLK):
                    for t in range(TT):
                        pool.wait_ge(s_ve[1], i + t)
                        pool.tensor_tensor(rstd[1][:, t:t + 1], ve[1][:, t:t + 1], half[:, t:t + 1], ALU.pow)\
                            .then_inc(s_rstd[1], 1)
                elif second:
                    inverse_sqrt(1, i - 1)

            iterations(pool, body)

        @block.tensor
        def _(pe):
            def x_slice(par, part, kk, t0, n):
                src = xT[par][part][:, :, kk % KT, :]
                off = SEQ_PAD - 1 if kk < KT else SEQ_PAD
                if t0 is None:
                    return src[:, :, off:off + SEQ]
                return src[:, t0 // SEQ, off + t0 % SEQ:off + t0 % SEQ + n]

            PARTS = ((0, 0), (0, 1), (1, 0))
            MOVING_LO_LAST = ((0, 0), (1, 0), (0, 1))

            def as_c_tiles(b):
                return bank[b][:, :].rearrange("p (c x) -> p c x", c=KT)

            def act_product(i, par, c):
                n = 0
                for a, b in MOVING_LO_LAST:
                    if c == 0 and b == 1:
                        pe.wait_ge(s_xT[par][1], 16 * i + (16 if par else 32))
                    for k in range(2 * KT):
                        ins = pe.matmul(bank[4 + c][:, :].rearrange("p (s t) -> p s t", s=NSEQ),
                                        wact_t[a][:, c, k, :], x_slice(par, b, k, None, 0),
                                        start=(n == 0), stop=(n == 6 * KT - 1))
                        n += 1
                ins.then_inc(s_aps, 1)

            def val_product(t):
                n = 0
                for k in range(KT):
                    for a, b in PARTS:
                        ins = pe.matmul(as_c_tiles(t), kv[a][:, k // 2, k % 2, t * P:(t + 1) * P],
                                        wval_t[b][:, :, k, :], start=(n == 0), stop=(n == 3 * KT - 1))
                        n += 1
                ins.then_inc(s_vps, 1)

            def rec_product(par, t, start):
                n = 0
                for a, b in MOVING_LO_LAST:
                    if start and t == 0 and a == 0:
                        pe.wait_ge(s_wrecT[b], 32)
                    for k in range(2 * KT):
                        ins = pe.matmul(as_c_tiles(4 + t), x_slice(par, a, k, t * P, P),
                                        wrec_t[b][:, :, k, :], start=(n == 0), stop=(n == 6 * KT - 1))
                        n += 1
                ins.then_inc(s_rps, 1)

            def ffn_product(t):
                n = 0
                for k in range(KT):
                    for b in (0, 1):
                        ins = pe.matmul(as_c_tiles(t), qT[:, t, k, :],
                                        wffn_t[b][:, :, k, :], start=(n == 0), stop=(n == 2 * KT - 1))
                        n += 1
                ins.then_inc(s_fps, 1)

            def body(i, n):
                first, second, more = halves(i)
                start = is_block(i, 0)
                par = n % 2
                if start:
                    pe.wait_ge(s_idf, 2)
                    pe.wait_ge(s_idsf, 1)
                    pe.transpose(bank[7][:, 0:TOKENS // P], ids_f[:, :], ident[0:TOKENS // P, 0:TOKENS // P])\
                        .then_inc(s_idsT, 1)
                    pe.wait_ge(s_pad, 4)
                if first:
                    pe.wait_ge(s_xT[par][0], 16 * i + (16 if par else 32))
                    for c in range(KT):
                        if start:
                            pe.wait_ge(s_wactT[c], 32)
                        else:
                            pe.wait_ge(s_rsig, 4 * i - 3 + c)
                        act_product(i, par, c)
                if second:
                    pe.wait_ge(s_kvhi, 2 * i)
                    pe.wait_ge(s_kvlo, 2 * i)
                    if is_block(i, 1):
                        pe.wait_ge(s_wT[VAL_W], 32)
                    for t in range(TT):
                        if not is_block(i, 1):
                            pe.wait_ge(s_fin, 4 * i - 7 + t)
                        val_product(t)
                if first:
                    for t in range(TT):
                        pe.wait_ge(s_z, 4 * i + t + 1)
                        rec_product(par, t, start)
                if is_block(i, 1):
                    pe.wait_ge(s_wT[FFN_W], 32)
                if second:
                    for t in range(TT):
                        pe.wait_ge(s_qT[t], 16 * i)
                        ffn_product(t)

            iterations(pe, body)

        @block.scalar
        def _(act):
            def norm(n, slot, src, dst, done, t, u):
                act.activation(dst[:, u, :], src[:, slot, t, :], ACT.Identity,
                               bias=nbias[n][:, t:t + 1], scale=rstd[n][:, t:t + 1]).then_inc(done, 1)

            def weight_hi(w, c):
                act.wait_ge(s_sc, 4 * (column(w, c).start + 1))
                dst = parts(w, c, 1, 0)
                if w == VAL_W:
                    dst = dst.rearrange("p (r two q) -> p r two q", r=PAIRS, two=2)
                act.activation(dst, natural(w, c), ACT.Identity, scale=wscale[:, column(w, c)])\
                    .then_inc(s_whi, 1)

            def xn_hi(i, n):
                act.wait_ge(s_nb[0], i + 1)
                for u, t in enumerate(TILE_AT):
                    norm(0, n % 2, h, xn16[0], s_xhi, t, u)

            def keep_rows(i, n):
                if not is_block(i, 0) and not is_block(i, 1):
                    act.wait_ge(s_out[n % 2], 8 * i - 8 * (n % 2))
                act.activation(h1[:, n % 2, :, :], h[:, n % 2, :, :], ACT.Copy).then_inc(s_kept, 1)

            def rec_sigmoid(i, t):
                act.wait_ge(s_rps, 4 * i + t + 1)
                act.activation(r4[:, t, :], bank[4 + t][:, :], ACT.Sigmoid,
                               scale=unscale[:, column(REC_W)]).then_inc(s_rsig, 1)

            def fourth_power(i, g):
                act.wait_ge(s_rmax, 2 * i + g + 1)
                act.activation(r4[:, GROUPS[g], :], r4[:, GROUPS[g], :], ACT.Square).then_inc(s_r2, 1)
                act.wait_ge(s_r2, 2 * i + g + 1)
                act.activation(r4[:, GROUPS[g], :], r4[:, GROUPS[g], :], ACT.Square).then_inc(s_r4, 1)

            def body(i, n):
                first, second, more = halves(i)
                start = is_block(i, 0)
                if start:
                    for c in range(2):
                        weight_hi(ACT_W, c)
                    xn_hi(0, 0)
                    for c in range(2, KT):
                        weight_hi(ACT_W, c)
                    for c in range(KT):
                        weight_hi(REC_W, c)
                if first:
                    if second:
                        act.wait_ge(s_kvlo, 2 * i)
                    for p in range(PAIRS):
                        for c in range(2):
                            act.wait_ge(s_aps, 4 * i + 2 * p + c + 1)
                            act.activation(z[:, p, c, :], bank[4 + 2 * p + c][:, :], ACT.Sigmoid,
                                           scale=unscale[:, column(ACT_W, 2 * p + c)]).then_inc(s_z, 1)
                        if p == 0:
                            act.wait_ge(s_sd[p], SD * i + 1)
                            act.activation(ab[:, p, :, :], z[:, p, :, :], ACT.Square).then_inc(s_sa[p], 1)
                            if more:
                                xn_hi(i + 1, n + 1)
                            if is_block(i, 1):
                                for k in range(KT):
                                    weight_hi(FFN_W, k)
                    act.wait_ge(s_sd[1], SD * i + 1)
                    act.activation(ab[:, 1, :, :], z[:, 1, :, :], ACT.Square).then_inc(s_sa[1], 1)
                    for p in range(PAIRS):
                        act.activation(cd[:, p, :, :], z[:, p, :, :], ACT.Ln).then_inc(s_sa[p], 1)
                        act.wait_ge(s_sd[p], SD * i + 2)
                        act.activation(ab[:, p, 0, :], ab[:, p, 0, :], ACT.Ln).then_inc(s_sa[p], 1)
                    for p in range(PAIRS):
                        act.wait_ge(s_sd[p], SD * i + 3)
                        act.activation(cd[:, p, 0, :], cd[:, p, 0, :], ACT.Tanh, scale=0.5).then_inc(s_sa[p], 1)
                    for p in range(PAIRS):
                        act.wait_ge(s_sd[p], SD * i + 7)
                        act.activation(ab[:, p, 1, :], ab[:, p, 1, :], ACT.Exp, scale=0.5).then_inc(s_sa[p], 1)
                    if not start:
                        keep_rows(i, n)
                if second:
                    for t in range(TT):
                        if is_block(i, NBLK):
                            act.wait_ge(s_nb[1], i + t)
                        elif t == 0:
                            act.wait_ge(s_nb[1], i)
                        norm(1, (n - 1) % 2, h1, y, s_y, t, t)
                if first:
                    for p in range(PAIRS):
                        act.wait_ge(s_sa[p], SA * i + 4)
                        act.activation(cd[:, p, 0, :], cd[:, p, 0, :], ACT.Arctan).then_inc(s_sa[p], 1)
                    for t in range(TT if start else TT - 1):
                        rec_sigmoid(i, t)
                    if start:
                        act.wait_ge(s_wrecT[0], 32)
                        for c in range(KT):
                            weight_hi(VAL_W, c)
                        act.wait_ge(s_wlo, 2 * KT)
                        keep_rows(i, n)
                    for p in range(PAIRS):
                        act.wait_ge(s_sd[p], SD * i + 13)
                        act.activation(cd[:, p, 1, :], cd[:, p, 0, :], ACT.Abs).then_inc(s_sa[p], 1)
                    for p in range(PAIRS):
                        act.activation(z[:, p, 1, :], cd[:, p, 0, :], ACT.Sin).then_inc(s_sa[p], 1)
                        act.wait_ge(s_sa[p], SA * i + 7)
                        act.activation(z[:, p, 0, :], cd[:, p, 1, :], ACT.Sin, bias=half_pi[:, :],
                                       scale=-1.0).then_inc(s_sa[p], 1)
                    for p in range(PAIRS):
                        act.wait_ge(s_sd[p], SD * i + SD)
                        act.activation(kv[0][:, p, :, :], z[:, p, :, :], ACT.Copy).then_inc(s_kvhi, 1)
                    fourth_power(i, 0)
                    if not start:
                        rec_sigmoid(i, TT - 1)
                    fourth_power(i, 1)

            act.wait_ge(s_const, 2)
            iterations(act, body)

        @block.vector
        def _(dve):
            def scan(p, out_c, out_h, data0, data1, initial, op0, op1):
                for s in range(NSEQ):
                    cols = slice(s * SEQ, (s + 1) * SEQ)
                    dve.tensor_tensor_scan(out_c[:, p, out_h, cols], data0[:, cols],
                                           data1[:, cols] if data1 is not None else step_row[:, :],
                                           initial, op0, op1).then_inc(s_sd[p], 1)

            def norm_stats(i, n, slot, src):
                for t in range(TT):
                    if is_block(i, 0):
                        dve.wait_ge(s_first_rows[t], 16)
                    dve.bn_stats(stats[n][:, t, :], src[:, slot, t, :]).then_inc(s_bn[n], 1)

            def norm_var(n, i, eps_scale):
                dve.wait_ge(s_bn[n], 4 * i + 4)
                dve.sem_inc(s_held[1], 1)
                for t in range(TT):
                    dve.bn_aggr(mv[n][:, t, :], stats[n][:, t, :]).then_inc(s_mv[n], 1)
                dve.wait_ge(s_mv[n], 4 * i + 4)
                dve.tensor_scalar(ve[n][:, :], mv[n][:, :, 1], EPS, eps_scale, ALU.add, ALU.mult)\
                    .then_inc(s_ve[n], 1)

            def norm_bias(n, i):
                dve.wait_ge(s_rstd[n], i + 1)
                dve.scalar_tensor_tensor(nbias[n][:, :], mv[n][:, :, 0], -1.0, rstd[n][:, :],
                                         ALU.mult, ALU.mult).then_inc(s_nb[n], 1)

            def weight_scale(one):
                j = one.start
                dve.tensor_scalar(amax_pos[:, one], amax_all[:, one], 1e-30, None, ALU.max).then_inc(s_sc, 1)
                dve.wait_ge(s_sc, 4 * j + 1)
                dve.tensor_scalar(pow2[:, one].bitcast(I32), amax_pos[:, one].bitcast(I32), EXP_MASK, None,
                                  ALU.bitwise_and).then_inc(s_sc, 1)
                dve.wait_ge(s_sc, 4 * j + 2)
                dve.tensor_scalar(wscale[:, one].bitcast(I32), pow2[:, one].bitcast(I32), -1.0,
                                  float((2 * 127 + W_EXP) << 23), ALU.mult, ALU.add).then_inc(s_sc, 1)
                dve.tensor_scalar(unscale[:, one], pow2[:, one], UNSCALE[j], None, ALU.mult).then_inc(s_sc, 1)

            def row_scale(c):
                dve.wait_ge(s_wact[c], 16)
                largest(amax_all[:, column(ACT_W, c)], wact_n[:, c, :], s_rowmax)
                dve.wait_ge(s_rowmax, c + 1)
                weight_scale(column(ACT_W, c))

            def matrix_scale(w):
                dve.wait_ge(s_amaxall, w)
                weight_scale(column(w))

            def weight_lo(w, c):
                dve.wait_ge(s_sc, 4 * (column(w, c).start + 1))
                dve.wait_ge(s_whi, KT * w + c + 1)
                hi, lo = parts(w, c, 1, 0), parts(w, c, 1, 1)
                if w == VAL_W:
                    hi, lo = [v.rearrange("p (r two q) -> p r two q", r=PAIRS, two=2) for v in (hi, lo)]
                    for r in range(PAIRS):
                        ins = dve.scalar_tensor_tensor(lo[:, r], natural(w, c)[:, r], wscale[:, column(w)],
                                                       hi[:, r], ALU.mult, ALU.subtract)
                    ins.then_inc(s_wlo, 1)
                    return
                dve.scalar_tensor_tensor(lo, natural(w, c), wscale[:, column(w, c)], hi,
                                         ALU.mult, ALU.subtract).then_inc(s_wlo, 1)

            def largest(dst, src, done):
                dve.tensor_reduce(dst, src, AX.X, ALU.max, apply_absolute_value=True).then_inc(done, 1)

            def xn_split(i, n):
                for u, t in enumerate(TILE_AT):
                    dve.tensor_scalar(xn[:, u, :], h[:, n % 2, t, :], rstd[0][:, t:t + 1], nbias[0][:, t:t + 1],
                                      ALU.mult, ALU.add).then_inc(s_xn, 1)
                for u in range(TT):
                    dve.wait_ge(s_xn, 4 * i + u + 1)
                    dve.wait_ge(s_xhi, 4 * i + u + 1)
                    dve.tensor_tensor(xn16[1][:, u, :], xn[:, u, :], xn16[0][:, u, :], ALU.subtract)\
                        .then_inc(s_xlo, 1)

            def clamp_z(p, i):
                dve.wait_ge(s_z, 4 * i + 2 * p + 2)
                dve.tensor_scalar(z[:, p, :, :], z[:, p, :, :], 0.5, None, ALU.max).then_inc(s_sd[p], 1)

            def square_z(p, i):
                dve.wait_ge(s_sa[p], SA * i + 1)
                dve.tensor_tensor(ab[:, p, 0, :], ab[:, p, 0, :], ab[:, p, 1, :], ALU.add).then_inc(s_sd[p], 1)

            def product_modulus(p, i):
                dve.wait_ge(s_sa[p], SA * i + 2)
                dve.tensor_tensor(cd[:, p, 0, :], cd[:, p, 1, :], cd[:, p, 0, :], ALU.subtract)\
                    .then_inc(s_sd[p], 1)
                dve.wait_ge(s_sa[p], SA * i + 3)
                scan(p, ab, 1, ab[:, p, 0, :], ab[:, p, 0, :], -1e30, ALU.max, ALU.max)
                dve.wait_ge(s_sd[p], SD * i + 5)
                scan(p, ab, 1, ab[:, p, 0, :], ab[:, p, 1, :], 0.0, ALU.add, ALU.subtract)

            def product_angle(i):
                for p in range(PAIRS):
                    dve.wait_ge(s_sa[p], SA * i + 6)
                    scan(p, cd, 1, cd[:, p, 0, :], None, 0.0, ALU.add, ALU.add)
                for p in range(PAIRS):
                    dve.wait_ge(s_sd[p], SD * i + 9)
                    dve.tensor_scalar(cd[:, p, 0, :], cd[:, p, 1, :], 1 / TWO_PI, MAGIC, ALU.mult, ALU.add)\
                        .then_inc(s_sd[p], 1)
                for p in range(PAIRS):
                    dve.wait_ge(s_sd[p], SD * i + 10)
                    dve.tensor_scalar(cd[:, p, 0, :], cd[:, p, 0, :], MAGIC, -TWO_PI, ALU.subtract, ALU.mult)\
                        .then_inc(s_sd[p], 1)
                for p in range(PAIRS):
                    dve.wait_ge(s_sd[p], SD * i + 11)
                    dve.tensor_tensor(cd[:, p, 0, :], cd[:, p, 0, :], cd[:, p, 1, :], ALU.add)\
                        .then_inc(s_sd[p], 1)
                for p in range(PAIRS):
                    dve.wait_ge(s_sd[p], SD * i + 12)
                    dve.tensor_scalar(cd[:, p, 0, :], cd[:, p, 0, :], PI_IN, -PI_IN, ALU.min, ALU.max)\
                        .then_inc(s_sd[p], 1)

            def product_parts(i):
                for p in range(PAIRS):
                    dve.wait_ge(s_sa[p], SA * i + SA)
                    for c in range(2):
                        ins = dve.scalar_tensor_tensor(z[:, p, c, :], ab[:, p, 1, :], KV_SCALE, z[:, p, c, :],
                                                       ALU.mult, ALU.mult)
                    ins.then_inc(s_sd[p], 1)
                for p in range(PAIRS):
                    dve.wait_ge(s_kvhi, 2 * i + p + 1)
                    dve.tensor_tensor(kv[1][:, p, :, :], z[:, p, :, :], kv[0][:, p, :, :], ALU.subtract)\
                        .then_inc(s_kvlo, 1)

            def ffn_levels():
                dve.wait_ge(s_wffn, 16)
                dve.tensor_scalar(level, wffn_n, W_THRESHOLD, W_LEVEL, ALU.is_gt, ALU.mult).then_inc(s_lvl, 1)
                dve.wait_ge(s_lvl, 1)
                dve.tensor_scalar(wffn_n, wffn_n, -W_THRESHOLD, -W_LEVEL, ALU.is_lt, ALU.mult).then_inc(s_lvl, 1)

            def load_start():
                dve.memset(half_pi[:, :], HALF_PI).then_inc(s_const, 1)
                for b in range(2):
                    for a in range(2):
                        dve.memset(xT[b][a][:, :, :, 0:SEQ_PAD], 0.0).then_inc(s_pad, 1)
                dve.wait_ge(s_ids, 16)
                dve.tensor_copy(ids_f[:, :], ids_i[:, :]).then_inc(s_idsf, 1)
                dve.wait_ge(s_idsT, 1)
                dve.tensor_scalar(over[:, :], bank[7][:, 0:TOKENS // P], float(VOCAB - EXTRA), float(EXTRA),
                                  ALU.is_ge, ALU.mult).then_inc(s_over, 1)
                dve.wait_ge(s_over, 1)
                dve.tensor_tensor(rows[:, :], bank[7][:, 0:TOKENS // P], over[:, :], ALU.add)\
                    .then_inc(s_rows, 1)
                for c in range(2):
                    row_scale(c)
                norm_stats(0, 0, 0, h)
                norm_var(0, 0, X_SCALE ** -2)
                weight_lo(ACT_W, 0)
                norm_bias(0, 0)
                dve.wait_ge(s_nb[0], 1)
                xn_split(0, 0)
                weight_lo(ACT_W, 1)
                for c in range(2, KT):
                    row_scale(c)
                for c in range(2, KT):
                    weight_lo(ACT_W, c)
                for c in range(KT):
                    dve.wait_ge(s_wrec[c], 16)
                    largest(chunk_max[:, c:c + 1], wrec_n[:, c, :], s_chunk)
                dve.wait_ge(s_chunk, KT)
                largest(amax[:, column(REC_W)], chunk_max[:, :], s_amax)
                matrix_scale(REC_W)
                for c in range(KT):
                    weight_lo(REC_W, c)

            def clamp_r(i, g):
                dve.wait_ge(s_rsig, 4 * i + GROUPS[g].stop)
                dve.tensor_scalar(r4[:, GROUPS[g], :], r4[:, GROUPS[g], :], 0.5, None, ALU.max)\
                    .then_inc(s_rmax, 1)

            def residual(i, t, old):
                if t in (0, TT - 1):
                    dve.wait_ge(s_r4, 2 * i - (t == 0))
                dve.wait_ge(s_vps, 4 * i - 4 + t + 1)
                dve.scalar_tensor_tensor(r4[:, t, :], bank[t][:, :], unscale[:, column(VAL_W)],
                                         r4[:, t, :], ALU.mult, ALU.mult).then_inc(s_t, 1)
                dve.wait_ge(s_t, 4 * i - 4 + t + 1)
                dve.tensor_tensor(h1[:, old, t, :], h1[:, old, t, :], r4[:, t, :], ALU.add)\
                    .then_inc(s_h1, 1)
                dve.wait_ge(s_h1, 4 * i - 4 + t + 1)
                dve.bn_stats(stats[1][:, t, :], h1[:, old, t, :]).then_inc(s_bn[1], 1)

            def ternary(i, t):
                dve.wait_ge(s_y, 4 * i - 4 + t + 1)
                dve.tensor_scalar(below[:, t, :], y[:, t, :], -X_THRESHOLD, None, ALU.is_lt)\
                    .then_inc(s_below, 1)
                dve.wait_ge(s_below, 4 * i - 4 + t + 1)
                dve.scalar_tensor_tensor(q[:, t, :], y[:, t, :], X_THRESHOLD, below[:, t, :],
                                         ALU.is_gt, ALU.subtract).then_inc(s_q, 1)

            def tile_var(i, t):
                dve.wait_ge(s_bn[1], 4 * i - 4 + t + 1)
                dve.bn_aggr(mv[1][:, t, :], stats[1][:, t, :]).then_inc(s_mv[1], 1)
                dve.wait_ge(s_mv[1], 4 * i - 4 + t + 1)
                dve.tensor_scalar(ve[1][:, t:t + 1], mv[1][:, t, 1:2], EPS, None, ALU.add).then_inc(s_ve[1], 1)

            def tile_bias(i, t):
                dve.wait_ge(s_rstd[1], i + t)
                dve.scalar_tensor_tensor(nbias[1][:, t:t + 1], mv[1][:, t, 0:1], -1.0, rstd[1][:, t:t + 1],
                                         ALU.mult, ALU.mult).then_inc(s_nb[1], 1)

            def finals(i, old):
                for t in range(TT):
                    dve.wait_ge(s_fps, 4 * i - 4 + t + 1)
                    dve.scalar_tensor_tensor(h1[:, old, t, :], bank[t][:, :], unscale[:, column(FFN_W)],
                                             h1[:, old, t, :], ALU.mult, ALU.add).then_inc(s_fin, 1)

            def body(i, n):
                first, second, more = halves(i)
                start = is_block(i, 0)
                old = (n - 1) % 2
                if start:
                    load_start()
                if more:
                    dve.wait_ge(s_gath[(n + 1) % 2], 32 * i + (32 if n % 2 else 64))
                    norm_stats(i + 1, 0, (n + 1) % 2, h)
                    norm_var(0, i + 1, X_SCALE ** -2)
                    norm_bias(0, i + 1)
                if is_block(i, 1):
                    matrix_scale(FFN_W)
                if first:
                    clamp_z(0, i)
                    square_z(0, i)
                if more:
                    xn_split(i + 1, n + 1)
                if is_block(i, 1):
                    weight_lo(FFN_W, 0)
                    weight_lo(FFN_W, 1)
                if first:
                    clamp_z(1, i)
                if is_block(i, 1):
                    weight_lo(FFN_W, 2)
                if first:
                    square_z(1, i)
                if is_block(i, 1):
                    weight_lo(FFN_W, 3)
                if first:
                    product_modulus(0, i)
                    product_modulus(1, i)
                if start:
                    dve.wait_ge(s_wval, 16)
                    largest(amax[:, column(VAL_W)], w_stage[:, 0:2048], s_amax)
                    ffn_levels()
                    matrix_scale(VAL_W)
                if second:
                    dve.wait_ge(s_kept, i)
                    if first:
                        for t in range(TT):
                            residual(i, t, old)
                        norm_var(1, i - 1, 1.0)
                        norm_bias(1, i - 1)
                        for t in range(TT):
                            ternary(i, t)
                    else:
                        for t in range(TT):
                            residual(i, t, old)
                            tile_var(i, t)
                            if t > 0:
                                tile_bias(i, t - 1)
                            if t > 1:
                                ternary(i, t - 2)
                        tile_bias(i, TT - 1)
                        ternary(i, TT - 2)
                        ternary(i, TT - 1)
                if start:
                    dve.wait_ge(s_steps, 16)
                if first:
                    product_angle(i)
                if start:
                    for c in range(KT):
                        weight_lo(VAL_W, c)
                if first:
                    clamp_r(i, 0)
                    product_parts(i)
                if second:
                    finals(i, old)
                if first:
                    clamp_r(i, 1)
                if start:
                    dve.wait_ge(s_lvl, 4)
                    largest(amax[:, column(FFN_W)], wvar_n, s_amax)

            iterations(dve, body)


def kernel(x, L0_tok_weight, L0_tok_extra, L0_attn_W_act, L0_attn_W_val, L0_attn_W_rec, L0_ffn_weight,
           L0_ffn_rram_variation):
    import concourse.bacc as bacc
    from concourse.bass_utils import run_bass_kernel_spmd

    arrays = {
        "ids": np.ascontiguousarray(x),
        "table": np.concatenate([np.asarray(L0_tok_weight), np.asarray(L0_tok_extra)], axis=0),
        "w_act": np.ascontiguousarray(L0_attn_W_act),
        "w_val": np.ascontiguousarray(L0_attn_W_val),
        "w_rec": np.ascontiguousarray(L0_attn_W_rec),
        "w_ffn": np.ascontiguousarray(L0_ffn_weight),
        "w_var": np.ascontiguousarray(L0_ffn_rram_variation),
        "steps": np.ascontiguousarray(np.broadcast_to(phase_steps(), (P, SEQ))),
    }
    nc = bacc.Bacc("TRN2", target_bir_lowering=False, num_devices=1)
    args = [nc.dram_tensor(name, a.shape, mybir.dt.from_np(a.dtype), kind="ExternalInput").ap()
            for name, a in arrays.items()]
    out = nc.dram_tensor("out", (BATCH, SEQ, DIM), F32, kind="ExternalOutput").ap()
    tower_kernel(nc, *args, out)
    result = run_bass_kernel_spmd(nc, [arrays], core_ids=[0])
    return result.results[0]["out"]
```
